# Optimizing a Trainium2 kernel written in Bass

```python
import numpy as np
import jax
import jax.numpy as jnp

def _softmax(x, axis=-1):
    return jax.nn.softmax(x, axis=axis)

def _gelu(x):
    return jax.nn.gelu(x, approximate=True)

def _silu(x):
    return jax.nn.silu(x)

def _sigmoid(x):
    return jax.nn.sigmoid(x)

def _layernorm(x, axis=-1, eps=1e-05):
    m = jnp.mean(x, axis=axis, keepdims=True)
    v = jnp.var(x, axis=axis, keepdims=True)
    return (x - m) / jnp.sqrt(v + eps)

def _scatter_add(tgt, idx, src, axis=0):
    return tgt.at[idx].add(src)

def _segment_sum(src, seg, n):
    return jax.ops.segment_sum(src, seg, n)
kernel_name = 'mk_flamingo_gated_d2_seqx_r8_b06e83'

def setup_inputs(seed: int=0):
    np.random.seed(seed)
    _w = jnp.asarray

    def _rec_inputs():
        import jax
        import jax.numpy as jnp
        _rk = jax.random.key(seed)
        x = 7.22e-05 + 1 * jax.random.normal(jax.random.fold_in(_rk, 1), (8, 256, 128), jnp.float32)
        _lenS = 256 - jax.random.randint(jax.random.fold_in(_rk, 7), (8,), 0, max(1, 256 // 4) + 1, jnp.int32)
        _lenS2 = 512 - jax.random.randint(jax.random.fold_in(_rk, 8), (8,), 0, max(1, 512 // 4) + 1, jnp.int32)
        _ctx_1024P = jax.random.normal(jax.random.fold_in(_rk, 11), (8, 16, 128), jnp.float32)
        _ctx_1024c = jax.random.dirichlet(jax.random.fold_in(_rk, 511), 0.3 * jnp.ones((16,), jnp.float32), (8, 512))
        _ctx_1024t = jnp.einsum('bsk,bkd->bsd', _ctx_1024c, _ctx_1024P)
        _ctx_1024t = _ctx_1024t * jax.lax.rsqrt(jnp.mean(jnp.square(_ctx_1024t)) + 1e-12) * 0.953939
        ctx_1024 = 4.13588e-05 + 0.999923 * (_ctx_1024t + 0.3 * jax.random.normal(jax.random.fold_in(_rk, 611), (8, 512, 128), jnp.float32))
        _g = jax.random.normal(jax.random.fold_in(_rk, 9001), (2, 2), jnp.float32)
        _g = jnp.sign(_g) * jnp.maximum(jnp.abs(_g), 1.0) + (_g == 0) * 1.0
        g_xattn = _g[0]
        g_ffn = _g[1]
        return (x, ctx_1024, g_xattn, g_ffn)
    x, ctx_1024, g_xattn, g_ffn = _rec_inputs()

    def _L0_xattn_setup():
        import jax, jax.numpy as jnp
        import numpy as np
        DIM = 128
        HEADS = 16
        HEAD_DIM = DIM // HEADS
        key = jax.random.key(seed)
        ks = jax.random.split(key, 11)
        B, Sq, Skv = (4, 256, 256)
        s = 1.0 / np.sqrt(DIM)
        return {'query': jax.random.normal(ks[0], (B, Sq, DIM), jnp.float32), 'key': jax.random.normal(ks[1], (B, Skv, DIM), jnp.float32), 'value': jax.random.normal(ks[2], (B, Skv, DIM), jnp.float32), 'Wq': jax.random.normal(ks[3], (DIM, DIM), jnp.float32) * s, 'bq': jnp.zeros((DIM,), jnp.float32), 'Wk': jax.random.normal(ks[4], (DIM, DIM), jnp.float32) * s, 'bk': jnp.zeros((DIM,), jnp.float32), 'Wv': jax.random.normal(ks[5], (DIM, DIM), jnp.float32) * s, 'bv': jnp.zeros((DIM,), jnp.float32), 'Wo': jax.random.normal(ks[6], (DIM, DIM), jnp.float32) * s, 'bo': jnp.zeros((DIM,), jnp.float32)}
    _L0_xattn_all = _L0_xattn_setup()
    _L0_xattn_in = {k: v for k, v in _L0_xattn_all.items() if k in ('Wq', 'bq', 'Wk', 'bk', 'Wv', 'bv', 'Wo', 'bo')}
    del _L0_xattn_all

    def _L0_ffn_setup():
        import jax, jax.numpy as jnp
        import numpy as np
        B, S, D, H, E = (4, 256, 128, 512, 8)
        key = jax.random.key(seed)
        ks = jax.random.split(key, 8)
        s_d = 1.0 / np.sqrt(D)
        s_h = 1.0 / np.sqrt(H)
        return {'x': jax.random.normal(ks[0], (B, S, D), dtype=jnp.float32), 'gate_w': jax.random.uniform(ks[1], (E, D), jnp.float32, -s_d, s_d), 'gate_b': jax.random.uniform(ks[2], (E,), jnp.float32, -s_d, s_d), 'w1': jax.random.uniform(ks[3], (E, H, D), jnp.float32, -s_d, s_d), 'b1': jax.random.uniform(ks[4], (E, H), jnp.float32, -s_d, s_d), 'w2': jax.random.uniform(ks[5], (E, D, H), jnp.float32, -s_h, s_h), 'b2': jax.random.uniform(ks[6], (E, D), jnp.float32, -s_h, s_h)}
    _L0_ffn_all = _L0_ffn_setup()
    _L0_ffn_in = {k: v for k, v in _L0_ffn_all.items() if k in ('gate_w', 'gate_b', 'w1', 'b1', 'w2', 'b2')}
    del _L0_ffn_all

    def _L1_xattn_setup():
        import jax, jax.numpy as jnp
        import numpy as np
        D = 128
        H = 16
        HD = D // H
        FFN = 512
        EPS = 1e-05

        def _mha(q_in, k_in, v_in, wq, bq, wk, bk, wv, bv):
            B, Sq, _ = q_in.shape
            Sk = k_in.shape[1]

            def split(x, S):
                return x.reshape(B, S, H, HD).transpose(0, 2, 1, 3)
            Q = split(q_in @ wq + bq, Sq)
            K = split(k_in @ wk + bk, Sk)
            V = split(v_in @ wv + bv, Sk)
            scores = jnp.einsum('bhqd,bhkd->bhqk', Q, K) / HD ** 0.5
            probs = jax.nn.softmax(scores, axis=-1)
            ctx = jnp.einsum('bhqk,bhkd->bhqd', probs, V)
            return ctx.transpose(0, 2, 1, 3).reshape(B, Sq, D)

        def _ln(x, g, b):
            mu = jnp.mean(x, axis=-1, keepdims=True)
            var = jnp.mean(jnp.square(x - mu), axis=-1, keepdims=True)
            return (x - mu) * jax.lax.rsqrt(var + EPS) * g + b
        key = jax.random.key(seed)
        ks = jax.random.split(key, 24)
        s = 1.0 / np.sqrt(D)
        inp = {'hidden_states': jax.random.normal(ks[0], (2, 256, D), jnp.float32), 'encoder_hidden_states': jax.random.normal(ks[1], (2, 256, D), jnp.float32), 'sa_wq': jax.random.normal(ks[2], (D, D), jnp.float32) * s, 'sa_bq': jnp.zeros((D,), jnp.float32), 'sa_wk': jax.random.normal(ks[3], (D, D), jnp.float32) * s, 'sa_bk': jnp.zeros((D,), jnp.float32), 'sa_wv': jax.random.normal(ks[4], (D, D), jnp.float32) * s, 'sa_bv': jnp.zeros((D,), jnp.float32), 'ln1_g': jnp.ones((D,), jnp.float32), 'ln1_b': jnp.zeros((D,), jnp.float32), 'ca_wq': jax.random.normal(ks[5], (D, D), jnp.float32) * s, 'ca_bq': jnp.zeros((D,), jnp.float32), 'ca_wk': jax.random.normal(ks[6], (D, D), jnp.float32) * s, 'ca_bk': jnp.zeros((D,), jnp.float32), 'ca_wv': jax.random.normal(ks[7], (D, D), jnp.float32) * s, 'ca_bv': jnp.zeros((D,), jnp.float32), 'ln2_g': jnp.ones((D,), jnp.float32), 'ln2_b': jnp.zeros((D,), jnp.float32), 'fc1_w': jax.random.normal(ks[8], (D, FFN), jnp.float32) * s, 'fc1_b': jnp.zeros((FFN,), jnp.float32), 'fc2_w': jax.random.normal(ks[9], (FFN, D), jnp.float32) * (1.0 / np.sqrt(FFN)), 'fc2_b': jnp.zeros((D,), jnp.float32), 'ln3_g': jnp.ones((D,), jnp.float32), 'ln3_b': jnp.zeros((D,), jnp.float32)}
        return inp
    _L1_xattn_all = _L1_xattn_setup()
    _L1_xattn_in = {k: v for k, v in _L1_xattn_all.items() if k in ('sa_wq', 'sa_bq', 'sa_wk', 'sa_bk', 'sa_wv', 'sa_bv', 'ln1_g', 'ln1_b', 'ca_wq', 'ca_bq', 'ca_wk', 'ca_bk', 'ca_wv', 'ca_bv', 'ln2_g', 'ln2_b', 'fc1_w', 'fc1_b', 'fc2_w', 'fc2_b', 'ln3_g', 'ln3_b')}
    del _L1_xattn_all

    def _L1_ffn_setup():
        import jax, jax.numpy as jnp
        import numpy as np
        DIM = 128
        N_HEADS = 16
        N_KV_HEADS = 4
        HEAD_DIM = DIM // N_HEADS
        N_REP = N_HEADS // N_KV_HEADS
        N_EXPERTS = 4
        TOP_K = 2
        HIDDEN = 3 * DIM
        EPS = 1.1920928955078125e-07

        def _rmsnorm(x, g):
            var = jnp.mean(jnp.square(x), axis=-1, keepdims=True)
            return x * jax.lax.rsqrt(var + EPS) * g

        def _rotate_half(x):
            x1, x2 = jnp.split(x, 2, axis=-1)
            return jnp.concatenate([-x2, x1], axis=-1)

        def _rope_tables(S):
            inv_freq = 1.0 / 10000.0 ** (jnp.arange(0, HEAD_DIM, 2, dtype=jnp.float32) / HEAD_DIM)
            freqs = jnp.arange(S, dtype=jnp.float32)[:, None] * inv_freq[None, :]
            emb = jnp.concatenate([freqs, freqs], axis=-1)
            return (jnp.cos(emb), jnp.sin(emb))

        def _attention(x, wq, wk, wv, wo):
            B, S, D = x.shape
            q = (x @ wq).reshape(B, S, N_HEADS, HEAD_DIM).transpose(0, 2, 1, 3)
            k = (x @ wk).reshape(B, S, N_KV_HEADS, HEAD_DIM).transpose(0, 2, 1, 3)
            v = (x @ wv).reshape(B, S, N_KV_HEADS, HEAD_DIM).transpose(0, 2, 1, 3)
            cos, sin = _rope_tables(S)
            q = q * cos + _rotate_half(q) * sin
            k = k * cos + _rotate_half(k) * sin
            k = jnp.repeat(k, N_REP, axis=1)
            v = jnp.repeat(v, N_REP, axis=1)
            scores = jnp.einsum('bhqd,bhkd->bhqk', q, k) / jnp.sqrt(jnp.float32(HEAD_DIM))
            causal = jnp.tril(jnp.ones((S, S), dtype=bool))
            scores = jnp.where(causal, scores, -jnp.inf)
            attn = jax.nn.softmax(scores, axis=-1)
            out = jnp.einsum('bhqk,bhkd->bhqd', attn, v)
            return out.transpose(0, 2, 1, 3).reshape(B, S, D) @ wo

        def _moe(x, gate, w1, w2, w3):
            B, S, D = x.shape
            xf = x.reshape(-1, D)
            probs = jax.nn.softmax(xf @ gate, axis=-1)
            w, idx = jax.lax.top_k(probs, TOP_K)
            w = w / jnp.sum(w, axis=-1, keepdims=True)
            oh = jax.nn.one_hot(idx, N_EXPERTS, dtype=xf.dtype)
            comb = jnp.einsum('nk,nke->ne', w, oh)
            out = jnp.zeros_like(xf)
            for e in range(N_EXPERTS):
                h = jax.nn.silu(xf @ w1[e]) * (xf @ w3[e])
                out = out + comb[:, e:e + 1] * (h @ w2[e])
            return out.reshape(B, S, D)
        key = jax.random.key(seed)
        ks = jax.random.split(key, 12)
        s = 0.02
        B, S = (2, 256)
        return {'x': jax.random.normal(ks[0], (B, S, DIM), jnp.float32), 'g1': jnp.ones((DIM,), jnp.float32), 'g2': jnp.ones((DIM,), jnp.float32), 'wq': jax.random.normal(ks[1], (DIM, N_HEADS * HEAD_DIM), jnp.float32) * s, 'wk': jax.random.normal(ks[2], (DIM, N_KV_HEADS * HEAD_DIM), jnp.float32) * s, 'wv': jax.random.normal(ks[3], (DIM, N_KV_HEADS * HEAD_DIM), jnp.float32) * s, 'wo': jax.random.normal(ks[4], (N_HEADS * HEAD_DIM, DIM), jnp.float32) * s, 'gate': jax.random.normal(ks[5], (DIM, N_EXPERTS), jnp.float32) * s, 'w1': jax.random.normal(ks[6], (N_EXPERTS, DIM, HIDDEN), jnp.float32) * s, 'w2': jax.random.normal(ks[7], (N_EXPERTS, HIDDEN, DIM), jnp.float32) * s, 'w3': jax.random.normal(ks[8], (N_EXPERTS, DIM, HIDDEN), jnp.float32) * s}
    _L1_ffn_all = _L1_ffn_setup()
    _L1_ffn_in = {k: v for k, v in _L1_ffn_all.items() if k in ('g1', 'g2', 'wq', 'wk', 'wv', 'wo', 'gate', 'w1', 'w2', 'w3')}
    del _L1_ffn_all
    return {'x': x, 'ctx_1024': ctx_1024, 'g_xattn': g_xattn, 'g_ffn': g_ffn, 'L0_xattn_Wq': _L0_xattn_in['Wq'], 'L0_xattn_bq': _L0_xattn_in['bq'], 'L0_xattn_Wk': _L0_xattn_in['Wk'], 'L0_xattn_bk': _L0_xattn_in['bk'], 'L0_xattn_Wv': _L0_xattn_in['Wv'], 'L0_xattn_bv': _L0_xattn_in['bv'], 'L0_xattn_Wo': _L0_xattn_in['Wo'], 'L0_xattn_bo': _L0_xattn_in['bo'], 'L0_ffn_gate_w': _L0_ffn_in['gate_w'], 'L0_ffn_gate_b': _L0_ffn_in['gate_b'], 'L0_ffn_w1': _L0_ffn_in['w1'], 'L0_ffn_b1': _L0_ffn_in['b1'], 'L0_ffn_w2': _L0_ffn_in['w2'], 'L0_ffn_b2': _L0_ffn_in['b2'], 'L1_xattn_sa_wq': _L1_xattn_in['sa_wq'], 'L1_xattn_sa_bq': _L1_xattn_in['sa_bq'], 'L1_xattn_sa_wk': _L1_xattn_in['sa_wk'], 'L1_xattn_sa_bk': _L1_xattn_in['sa_bk'], 'L1_xattn_sa_wv': _L1_xattn_in['sa_wv'], 'L1_xattn_sa_bv': _L1_xattn_in['sa_bv'], 'L1_xattn_ln1_g': _L1_xattn_in['ln1_g'], 'L1_xattn_ln1_b': _L1_xattn_in['ln1_b'], 'L1_xattn_ca_wq': _L1_xattn_in['ca_wq'], 'L1_xattn_ca_bq': _L1_xattn_in['ca_bq'], 'L1_xattn_ca_wk': _L1_xattn_in['ca_wk'], 'L1_xattn_ca_bk': _L1_xattn_in['ca_bk'], 'L1_xattn_ca_wv': _L1_xattn_in['ca_wv'], 'L1_xattn_ca_bv': _L1_xattn_in['ca_bv'], 'L1_xattn_ln2_g': _L1_xattn_in['ln2_g'], 'L1_xattn_ln2_b': _L1_xattn_in['ln2_b'], 'L1_xattn_fc1_w': _L1_xattn_in['fc1_w'], 'L1_xattn_fc1_b': _L1_xattn_in['fc1_b'], 'L1_xattn_fc2_w': _L1_xattn_in['fc2_w'], 'L1_xattn_fc2_b': _L1_xattn_in['fc2_b'], 'L1_xattn_ln3_g': _L1_xattn_in['ln3_g'], 'L1_xattn_ln3_b': _L1_xattn_in['ln3_b'], 'L1_ffn_g1': _L1_ffn_in['g1'], 'L1_ffn_g2': _L1_ffn_in['g2'], 'L1_ffn_wq': _L1_ffn_in['wq'], 'L1_ffn_wk': _L1_ffn_in['wk'], 'L1_ffn_wv': _L1_ffn_in['wv'], 'L1_ffn_wo': _L1_ffn_in['wo'], 'L1_ffn_gate': _L1_ffn_in['gate'], 'L1_ffn_w1': _L1_ffn_in['w1'], 'L1_ffn_w2': _L1_ffn_in['w2'], 'L1_ffn_w3': _L1_ffn_in['w3']}

def reference(x, ctx_1024, g_xattn, g_ffn, L0_xattn_Wq, L0_xattn_bq, L0_xattn_Wk, L0_xattn_bk, L0_xattn_Wv, L0_xattn_bv, L0_xattn_Wo, L0_xattn_bo, L0_ffn_gate_w, L0_ffn_gate_b, L0_ffn_w1, L0_ffn_b1, L0_ffn_w2, L0_ffn_b2, L1_xattn_sa_wq, L1_xattn_sa_bq, L1_xattn_sa_wk, L1_xattn_sa_bk, L1_xattn_sa_wv, L1_xattn_sa_bv, L1_xattn_ln1_g, L1_xattn_ln1_b, L1_xattn_ca_wq, L1_xattn_ca_bq, L1_xattn_ca_wk, L1_xattn_ca_bk, L1_xattn_ca_wv, L1_xattn_ca_bv, L1_xattn_ln2_g, L1_xattn_ln2_b, L1_xattn_fc1_w, L1_xattn_fc1_b, L1_xattn_fc2_w, L1_xattn_fc2_b, L1_xattn_ln3_g, L1_xattn_ln3_b, L1_ffn_g1, L1_ffn_g2, L1_ffn_wq, L1_ffn_wk, L1_ffn_wv, L1_ffn_wo, L1_ffn_gate, L1_ffn_w1, L1_ffn_w2, L1_ffn_w3):
    import jax
    import jax.numpy as jnp

    def _L0_xattn_ref(query, key, value, Wq, bq, Wk, bk, Wv, bv, Wo, bo):
        import jax, jax.numpy as jnp
        import numpy as np
        DIM = 128
        HEADS = 16
        HEAD_DIM = DIM // HEADS
        B = query.shape[0]
        scale = HEAD_DIM ** (-0.5)
        q = (query @ Wq.T + bq).reshape(B, -1, HEADS, HEAD_DIM)
        k = (key @ Wk.T + bk).reshape(B, -1, HEADS, HEAD_DIM)
        v = (value @ Wv.T + bv).reshape(B, -1, HEADS, HEAD_DIM)
        scores = jnp.einsum('bqhd,bkhd->bhqk', q, k) * scale
        attn = jax.nn.softmax(scores, axis=-1)
        out = jnp.einsum('bhqk,bkhd->bqhd', attn, v).reshape(B, -1, DIM)
        return out @ Wo.T + bo

    def _L0_ffn_ref(x, gate_w, gate_b, w1, b1, w2, b2):
        import jax, jax.numpy as jnp
        import numpy as np
        B, S, D, H, E = (4, 256, 128, 512, 8)
        b, s, d = x.shape
        xf = x.reshape(-1, d)
        logits = xf @ gate_w.T + gate_b
        top1 = jnp.argmax(logits, axis=-1)
        out = jnp.zeros_like(xf)
        n_experts = w1.shape[0]
        for e in range(n_experts):
            h = jax.nn.relu(xf @ w1[e].T + b1[e])
            y = h @ w2[e].T + b2[e]
            out = out + jnp.where((top1 == e)[:, None], y, jnp.zeros((), y.dtype))
        return out.reshape(b, s, d)

    def _L1_xattn_ref(hidden_states, encoder_hidden_states, sa_wq, sa_bq, sa_wk, sa_bk, sa_wv, sa_bv, ln1_g, ln1_b, ca_wq, ca_bq, ca_wk, ca_bk, ca_wv, ca_bv, ln2_g, ln2_b, fc1_w, fc1_b, fc2_w, fc2_b, ln3_g, ln3_b):
        import jax, jax.numpy as jnp
        import numpy as np
        D = 128
        H = 16
        HD = D // H
        FFN = 512
        EPS = 1e-05

        def _mha(q_in, k_in, v_in, wq, bq, wk, bk, wv, bv):
            B, Sq, _ = q_in.shape
            Sk = k_in.shape[1]

            def split(x, S):
                return x.reshape(B, S, H, HD).transpose(0, 2, 1, 3)
            Q = split(q_in @ wq + bq, Sq)
            K = split(k_in @ wk + bk, Sk)
            V = split(v_in @ wv + bv, Sk)
            scores = jnp.einsum('bhqd,bhkd->bhqk', Q, K) / HD ** 0.5
            probs = jax.nn.softmax(scores, axis=-1)
            ctx = jnp.einsum('bhqk,bhkd->bhqd', probs, V)
            return ctx.transpose(0, 2, 1, 3).reshape(B, Sq, D)

        def _ln(x, g, b):
            mu = jnp.mean(x, axis=-1, keepdims=True)
            var = jnp.mean(jnp.square(x - mu), axis=-1, keepdims=True)
            return (x - mu) * jax.lax.rsqrt(var + EPS) * g + b
        h = _mha(hidden_states, hidden_states, hidden_states, sa_wq, sa_bq, sa_wk, sa_bk, sa_wv, sa_bv)
        x = _ln(hidden_states + h, ln1_g, ln1_b)
        h = _mha(x, encoder_hidden_states, encoder_hidden_states, ca_wq, ca_bq, ca_wk, ca_bk, ca_wv, ca_bv)
        x = _ln(x + h, ln2_g, ln2_b)
        h = jax.nn.relu(x @ fc1_w + fc1_b) @ fc2_w + fc2_b
        return _ln(x + h, ln3_g, ln3_b)

    def _L1_ffn_ref(x, g1, g2, wq, wk, wv, wo, gate, w1, w2, w3):
        import jax, jax.numpy as jnp
        import numpy as np
        DIM = 128
        N_HEADS = 16
        N_KV_HEADS = 4
        HEAD_DIM = DIM // N_HEADS
        N_REP = N_HEADS // N_KV_HEADS
        N_EXPERTS = 4
        TOP_K = 2
        HIDDEN = 3 * DIM
        EPS = 1.1920928955078125e-07

        def _rmsnorm(x, g):
            var = jnp.mean(jnp.square(x), axis=-1, keepdims=True)
            return x * jax.lax.rsqrt(var + EPS) * g

        def _rotate_half(x):
            x1, x2 = jnp.split(x, 2, axis=-1)
            return jnp.concatenate([-x2, x1], axis=-1)

        def _rope_tables(S):
            inv_freq = 1.0 / 10000.0 ** (jnp.arange(0, HEAD_DIM, 2, dtype=jnp.float32) / HEAD_DIM)
            freqs = jnp.arange(S, dtype=jnp.float32)[:, None] * inv_freq[None, :]
            emb = jnp.concatenate([freqs, freqs], axis=-1)
            return (jnp.cos(emb), jnp.sin(emb))

        def _attention(x, wq, wk, wv, wo):
            B, S, D = x.shape
            q = (x @ wq).reshape(B, S, N_HEADS, HEAD_DIM).transpose(0, 2, 1, 3)
            k = (x @ wk).reshape(B, S, N_KV_HEADS, HEAD_DIM).transpose(0, 2, 1, 3)
            v = (x @ wv).reshape(B, S, N_KV_HEADS, HEAD_DIM).transpose(0, 2, 1, 3)
            cos, sin = _rope_tables(S)
            q = q * cos + _rotate_half(q) * sin
            k = k * cos + _rotate_half(k) * sin
            k = jnp.repeat(k, N_REP, axis=1)
            v = jnp.repeat(v, N_REP, axis=1)
            scores = jnp.einsum('bhqd,bhkd->bhqk', q, k) / jnp.sqrt(jnp.float32(HEAD_DIM))
            causal = jnp.tril(jnp.ones((S, S), dtype=bool))
            scores = jnp.where(causal, scores, -jnp.inf)
            attn = jax.nn.softmax(scores, axis=-1)
            out = jnp.einsum('bhqk,bhkd->bhqd', attn, v)
            return out.transpose(0, 2, 1, 3).reshape(B, S, D) @ wo

        def _moe(x, gate, w1, w2, w3):
            B, S, D = x.shape
            xf = x.reshape(-1, D)
            probs = jax.nn.softmax(xf @ gate, axis=-1)
            w, idx = jax.lax.top_k(probs, TOP_K)
            w = w / jnp.sum(w, axis=-1, keepdims=True)
            oh = jax.nn.one_hot(idx, N_EXPERTS, dtype=xf.dtype)
            comb = jnp.einsum('nk,nke->ne', w, oh)
            out = jnp.zeros_like(xf)
            for e in range(N_EXPERTS):
                h = jax.nn.silu(xf @ w1[e]) * (xf @ w3[e])
                out = out + comb[:, e:e + 1] * (h @ w2[e])
            return out.reshape(B, S, D)
        x = x + _attention(_rmsnorm(x, g1), wq, wk, wv, wo)
        x = x + _moe(_rmsnorm(x, g2), gate, w1, w2, w3)
        return x
    x = x + jnp.tanh(g_xattn[0]) * _L0_xattn_ref(_layernorm(x, axis=-1), ctx_1024, ctx_1024, L0_xattn_Wq, L0_xattn_bq, L0_xattn_Wk, L0_xattn_bk, L0_xattn_Wv, L0_xattn_bv, L0_xattn_Wo, L0_xattn_bo)
    x = x + jnp.tanh(g_ffn[0]) * _L0_ffn_ref(_layernorm(x, axis=-1), L0_ffn_gate_w, L0_ffn_gate_b, L0_ffn_w1, L0_ffn_b1, L0_ffn_w2, L0_ffn_b2)
    x = x + jnp.tanh(g_xattn[1]) * _L1_xattn_ref(_layernorm(x, axis=-1), ctx_1024, L1_xattn_sa_wq, L1_xattn_sa_bq, L1_xattn_sa_wk, L1_xattn_sa_bk, L1_xattn_sa_wv, L1_xattn_sa_bv, L1_xattn_ln1_g, L1_xattn_ln1_b, L1_xattn_ca_wq, L1_xattn_ca_bq, L1_xattn_ca_wk, L1_xattn_ca_bk, L1_xattn_ca_wv, L1_xattn_ca_bv, L1_xattn_ln2_g, L1_xattn_ln2_b, L1_xattn_fc1_w, L1_xattn_fc1_b, L1_xattn_fc2_w, L1_xattn_fc2_b, L1_xattn_ln3_g, L1_xattn_ln3_b)
    x = x + jnp.tanh(g_ffn[1]) * _L1_ffn_ref(_layernorm(x, axis=-1), L1_ffn_g1, L1_ffn_g2, L1_ffn_wq, L1_ffn_wk, L1_ffn_wv, L1_ffn_wo, L1_ffn_gate, L1_ffn_w1, L1_ffn_w2, L1_ffn_w3)
    return x

_drawn_inputs = setup_inputs


def setup_inputs(seed=0):
    import zlib

    import numpy as np

    out = dict(_drawn_inputs(seed))
    spreads = {'g_ffn': (-1.0, 0.2),
     'L0_xattn_bq': (0.0, 0.1),
     'L0_xattn_bk': (0.0, 0.8),
     'L0_xattn_bv': (0.0, 0.1),
     'L0_xattn_bo': (0.0, 0.1),
     'L1_xattn_sa_bq': (0.0, 0.8),
     'L1_xattn_sa_bk': (0.0, 0.8),
     'L1_xattn_sa_bv': (0.0, 0.1),
     'L1_xattn_ln1_g': (1.0, 0.2),
     'L1_xattn_ln1_b': (0.0, 0.1),
     'L1_xattn_ca_bq': (0.0, 0.445),
     'L1_xattn_ca_bk': (0.0, 0.8),
     'L1_xattn_ca_bv': (0.0, 0.1),
     'L1_xattn_ln2_g': (1.0, 0.2),
     'L1_xattn_ln2_b': (0.0, 0.1),
     'L1_xattn_fc1_b': (0.0, 0.1),
     'L1_xattn_fc2_b': (0.0, 0.1),
     'L1_xattn_ln3_g': (1.0, 0.2),
     'L1_xattn_ln3_b': (0.0, 0.1),
     'L1_ffn_g1': (1.0, 0.2),
     'L1_ffn_g2': (1.0, 0.6)}
    factors = {'L0_ffn_b1': 3.687, 'L1_ffn_wq': 8.0, 'L1_ffn_wk': 8.0}
    for name, (base, spread) in spreads.items():
        noise = np.random.default_rng([zlib.crc32(name.encode()), seed]).standard_normal(out[name].shape)
        drawn = base * np.exp(spread * noise) if base else spread * noise
        out[name] = jnp.asarray(drawn.astype(out[name].dtype))
    for name, factor in factors.items():
        out[name] = (out[name] * factor).astype(out[name].dtype)
    return out
```

```python
from contextlib import ExitStack

import numpy as np

import concourse.bass as bass
import concourse.mybir as mybir
from concourse.alu_op_type import AluOpType as ALU

F32 = mybir.dt.float32
BF16 = mybir.dt.bfloat16
ACT = mybir.ActivationFunctionType
AX = mybir.AxisListType

P = 128
D = 128
B = 8
SQ = 256
QT = SQ // P
SC = 512
HEADS = 16
HD = D // HEADS
PARTS = 3
ROWS = PARTS * PARTS * HD
MROW = 96
KROWS = MROW + PARTS
GH = 4
NG = HEADS // GH
VW = 32
SCALE = float(HD) ** -0.5
RING = 8
MAX_AT = 1
TWO_ONES = float(np.array(0x3F803F80, np.uint32).view(np.float32))
PARTS_AT, RES_AT, INPUTS_AT = 1, 4, 12
BIG = -1.0e30
E0, H0 = 8, 512
E1, H1 = 4, 384
HF = 512
BLK = 512
NBLK = B * SQ // BLK
BT = BLK // P
EPS = 1e-5
EPS_RMS = 1.1920928955078125e-07


class Lin:

    def __init__(self, k, m=0):
        self.k, self.m = k, m

    def __add__(self, o):
        return Lin(self.k + o.k, self.m + o.m) if isinstance(o, Lin) else Lin(self.k + o, self.m)

    def __sub__(self, o):
        return self + (-o)

    def __mul__(self, c):
        return Lin(self.k * c, self.m * c)

    def half(self):
        return Lin(self.k // 2, self.m // 2)

    def odd(self):
        return self.k % 2

    def on(self, j):
        return self.k if j is None or self.m == 0 else j * self.m + self.k


class Att:

    def __init__(self, n, name, keys, own_kv, rope, wo, tail):
        self.n, self.name, self.keys, self.own_kv, self.rope, self.wo, self.tail = n, name, keys, own_kv, rope, wo, tail
        self.kt = keys // P
        self.slots = HEADS * self.kt * SQ // 1024
        self.hps = HEADS // self.slots
        self.gs = self.slots // NG
        self.lead = 2 * self.gs + 1


ATTS = [
    Att(0, "att0", SC, False, False, True, "gate"),
    Att(1, "att1", SQ, True, False, False, "affine"),
    Att(2, "att2", SC, False, False, False, "affine"),
    Att(3, "att3", SQ, True, True, True, "rms"),
]
SLOT0 = [sum(a.slots for a in ATTS[:n]) * B for n in range(4)]
IN0 = [sum((1 if a.own_kv else 2) for a in ATTS[:n]) * 16 * B // 2 for n in range(4)]


def att_steps(a, misc0, split_post, last_post=()):
    gs, sl = a.gs, a.slots
    segs = []
    count = [misc0]

    def number(steps, iters):
        uses = sum(s[3] for s in steps)
        out = []
        for kind, b, arg, use in steps:
            out.append((kind, b, arg, Lin(count[0], uses if iters else 0) if use else None))
            count[0] += use
        if iters:
            count[0] += uses * (iters - 1)
        segs.append((iters, out))

    def s_units(b, s, out, u):
        out.append(("S", b, (s, u), 0))
        if u == 1 and s % gs == gs - 1:
            out.append(("maxsplit", b, s // gs, 0))

    def project(b):
        return [("q", b, None, 1), ("k", b, None, 1)]

    def output(b):
        it = {6: [("ctx", b, 0, 1)], 7: [("ctx", b, 1, 1)], 15: [("nT", b, None, 1)]}
        if a.wo:
            it[8] = [("aT", b, None, 1)]
            it[11] = [("proj", b, None, 1)]
            it[14] = [("apply", b, None, 0)]
        else:
            it[8] = [("resid", b, None, 0)]
            it[12] = [("apply", b, None, 0)]
        return it

    def body(b, first, left):
        items = {p: [] for p in range(16)}

        def put(p, *steps):
            items[p] += list(steps)

        put(MAX_AT, ("maxT", b, 1, 1))
        if left >= 1:
            put(PARTS_AT, ("loadqk", b + 1, None, 0))
        if not first:
            put(RES_AT, ("loadres", b - 1, None, 0))
        put(MAX_AT + 4, ("maxT", b, 2, 1))
        put(MAX_AT + 8, ("maxT", b, 3, 1))
        if left >= 1:
            put(MAX_AT + 12, ("maxT", b + 1, 0, 1))
        if left >= 2:
            put(2, ("q", b + 2, None, 1), ("qsplit", b + 2, None, 0))
            put(4, ("k", b + 2, None, 1), ("ksplit", b + 2, 0, 0))
            put(5, ("qstore", b + 2, None, 0))
            if a.kt > 2:
                put(9, ("ksplit", b + 2, 1, 0))
            put(10 if a.kt == 2 else 14, ("kstore", b + 2, None, 0))
        if not first:
            for p, st in output(b - 1).items():
                put(p, *st)
        if left >= 1:
            put(10, ("v", b + 1, None, 1))
        if left >= 3:
            put(INPUTS_AT, ("loadin", b + 3, None, 0))
        if b.m == 0 and a.n < 2:
            put(7, ("weights", b, None, 0))
        out = []
        for s in range(sl):
            out.append(("E", b, s, 0))
            t = s + a.lead
            lead = (b, t) if t < sl else (b + 1, t - sl)
            has = t < sl or left >= 1
            if has:
                s_units(*lead, out, 0)
            per = 16 // sl
            out += items[per * s]
            if s >= gs or not first:
                out.append(("AV", b if s >= gs else b - 1, ((s // gs - 1) % NG, s % gs), 0))
            if has:
                s_units(*lead, out, 1)
            if per == 2:
                out += items[per * s + 1]
        return out

    pre = [("loadin", Lin(b), None, 0) for b in range(2)]
    for b in range(2):
        pre += project(Lin(b)) + [("qsplit", Lin(b), None, 0), ("ksplit", Lin(b), 0, 0)]
        if a.kt > 2:
            pre.append(("ksplit", Lin(b), 1, 0))
        if last_post:
            old = [("before", st[1], (st[0], st[2]), st[3]) for st in last_post]
            if b == 0:
                at = len(pre) - 5
                pre[at:] = [pre[at], old[0], pre[at + 1], old[1], pre[at + 2], old[2]] + pre[at + 3:]
            else:
                at = len(pre) - 5
                pre[at:at] = old[3:4]
                pre += old[4:]
        if b == 0:
            pre += [("qstore", Lin(b), None, 0), ("kstore", Lin(b), None, 0), ("loadqk", Lin(0), None, 0),
                    ("v", Lin(0), None, 1), ("loadin", Lin(2), None, 0)]
    for s in range(a.lead):
        for u in range(2):
            s_units(Lin(0), s, pre, u)
    pre += [("qstore", Lin(1), None, 0), ("kstore", Lin(1), None, 0), ("maxT", Lin(0), 0, 1)]
    number(pre, None)
    number(body(Lin(0), True, 7), None)
    iters = (B - 4) // 2
    number(body(Lin(1, 2), False, 3) + body(Lin(2, 2), False, 3), iters)
    for b in range(2 * iters + 1, B):
        number(body(Lin(b), False, B - 1 - b), None)
    last = Lin(B - 1)
    post = [st for p, sts in sorted(output(last).items()) for st in sts]
    tail = [("loadres", last, None, 0)] + [("AV", last, (NG - 1, p), 0) for p in range(gs)]
    number(tail if split_post else tail + post, None)
    return segs, post, count[0]


def program(nc, dram, outs):
    es = ExitStack()
    with es:
        def sb(name, shape, dt=F32):
            return es.enter_context(nc.sbuf_tensor(name, shape, dt))

        def sem(name):
            return es.enter_context(nc.semaphore(name))

        def scratch(name, shape, dt=F32):
            return nc.dram_tensor(name, shape, dt, kind="Internal").ap()

        T = B * SQ
        feat = {n: scratch(f"feat_{n}", (P, T)) for n in ("att0", "moe0", "att1", "att2", "ffn", "att3", "moe1")}
        rows = {n: scratch(f"rows_{n}", (T, D)) for n in ("x1", "x2", "z", "y1", "y2", "x3", "z4", "u")}
        rows["x"], rows["out"] = dram["x"], outs[0]
        q_scr = scratch("q_parts", (2, PARTS, P, SQ), BF16)
        k_scr = scratch("k_parts", (2, 2 * PARTS - 1, P, SC), BF16)
        RES = {"att0": ("x", "x1"), "att1": ("z", "y1"), "att2": ("y1", "y2"), "att3": ("z4", "u")}
        NEXT = {"att0": "moe0", "att1": "att2", "att2": "ffn", "att3": "moe1"}

        e_ps = es.enter_context(nc.psum_tensor("e_ps", [P, 2, 1024], F32))
        s_ps = es.enter_context(nc.psum_tensor("s_ps", [P, 2, 512], F32))
        av_ps = es.enter_context(nc.psum_tensor("av_ps", [P, 512], F32))
        misc = es.enter_context(nc.psum_tensor("misc", [P, 512], F32))
        hid_ps = e_ps[:, :, :].rearrange("p a (b c) -> p (a b) c", b=2)

        ident = sb("ident", [P, P])
        identb = sb("identb", [P, P], BF16)
        wts = sb("wts", [P, 16, D])
        WI = {n: i for i, n in enumerate(("att0_q", "att0_k", "att0_v", "att0_o", "att1_q", "att1_k", "att1_v",
                                          "att2_q", "att2_k", "att2_v", "att3_q", "att3_qs", "att3_k", "att3_ks",
                                          "att3_v", "att3_o"))}
        vecs = sb("vecs", [P, 12, D])
        VI = {n: i for i, n in enumerate(("att0_bo", "att0_bv", "att1_bv", "att2_bv", "att1_g", "att1_b",
                                          "att2_g", "att2_b", "ffn_g", "ffn_b", "g1", "att3_g"))}
        cols = sb("cols", [P, 8])
        CI = {n: i for i, n in enumerate(("att0_q", "att0_k", "att1_q", "att1_k", "att2_q", "att2_k", "fc2_b"))}
        qbias = sb("qbias", [P, 8])
        gates = sb("gates", [P, 4])
        tg = sb("tg", [P, 4])
        GI = {"att0": 0, "ffn": 1, "moe0": 2, "moe1": 3}
        ropes = sb("ropes", [P, 4, SQ])
        mask_f = sb("mask_f", [P, 3, P])
        maskb = sb("maskb", [P, 3, P], BF16)
        nhalf = sb("nhalf", [P, BT])
        epss = sb("epss", [P, 2, BT])
        zeros = sb("zeros", [P, QT, GH])
        zero8 = zeros[:, :, :]
        wbig = sb("wbig", [P, 2 * E0 * H0])
        w1_0 = wbig[:, 0:E0 * H0].rearrange("p (e h) -> p e h", e=E0)
        w2_0 = wbig[:, E0 * H0:2 * E0 * H0].rearrange("p (e t d) -> p e t d", e=E0, t=H0 // P)
        w1_1 = wbig[:, 0:E1 * H1].rearrange("p (e h) -> p e h", e=E1)
        w3_1 = wbig[:, E1 * H1:2 * E1 * H1].rearrange("p (e h) -> p e h", e=E1)
        w2_1 = wbig[:, 2 * E1 * H1:3 * E1 * H1].rearrange("p (e t d) -> p e t d", e=E1, t=H1 // P)
        fc1 = wbig[:, 3 * E1 * H1:3 * E1 * H1 + HF]
        fc2 = wbig[:, 3 * E1 * H1 + HF:3 * E1 * H1 + 2 * HF].rearrange("p (t d) -> p t d", t=HF // P)
        b1_0 = sb("b1_0", [P, E0, H0 // P])
        b2_0 = sb("b2_0", [E0, D])
        gw0 = sb("gw0", [P, E0])
        gb0 = sb("gb0", [P, E0])
        iota = sb("iota", [P, E0])
        sel_f = sb("sel_f", [E0, E0, P])
        sel_b = sb("sel_b", [E0, E0, P], BF16)
        fc1b = sb("fc1b", [P, HF // P])
        gw1 = sb("gw1", [P, E1])

        Kst = sb("Kst", [P, 2, HEADS, SC], BF16)
        Qst = sb("Qst", [P, 2, HEADS, SQ], BF16)
        Vx = sb("Vx", [P, 2, SC // P, HEADS, VW])
        prob = sb("prob", [P, RING, 1024])
        OT = sb("OT", [P, 2, NG, SQ])
        inT = sb("inT", [P, 2, SQ])
        ctxT = sb("ctxT", [P, 2, SC])
        qk = sb("qk", [P, 3 * SC])
        kf, rk = qk[:, 0:SC], qk[:, SC:2 * SC]
        qf, rq = qk[:, 2 * SC:2 * SC + SQ], qk[:, 2 * SC + SQ:3 * SC]
        qp = sb("qp", [P, PARTS, SQ], BF16)
        kp = sb("kp", [P, PARTS, SC], BF16)
        rt = sb("rt", [P, 2, SQ])
        nmax = sb("nmax", [P, 4, QT, GH])
        mres = sb("mres", [P, 2, QT * GH])
        mparts = sb("mparts", [P, 4, QT, PARTS, GH], BF16)
        mrow = sb("mrow", [PARTS * GH, 2, SQ], BF16)
        rden = sb("rden", [P, HEADS])
        att = sb("att", [P, QT, D])
        aT = sb("aT", [P, SQ])
        res = sb("res", [P, 2, QT, D])
        newres = sb("newres", [P, 2, QT, D])
        normed = sb("normed", [P, 2, QT, D])
        nT = sb("nT", [P, SQ])
        stats = sb("stats", [P, BT, 6])
        mv = sb("mv", [P, BT, 2])
        rin = sb("rin", [P, BT])
        rstd = sb("rstd", [P, BT])

        hid = prob[:, 0:4, :].rearrange("p a (b c) -> p (a b) c", b=2)
        gated = prob[:, 4:8, :].rearrange("p a (b c) -> p (a b) c", b=2)
        fin = sb("fin", [P, 2, BLK])
        fres = OT[:, 0, :, :].rearrange("p a b -> p (a b)").rearrange("p (a t d) -> p a t d", a=2, t=BT)
        fres2 = OT[:, 1, :, :].rearrange("p a b -> p (a b)").rearrange("p (a t d) -> p a t d", a=2, t=BT)
        ft1, ft2, ft3 = (qk[:, SC * n:SC * n + SC].rearrange("p (t d) -> p t d", t=BT) for n in range(3))
        ysb, fT = ctxT[:, 0, :], ctxT[:, 1, :]
        lg = sb("lg", [P, BT, E0])
        lg2 = sb("lg2", [P, BT, E0])
        lg3 = sb("lg3", [P, BT, E0])
        lg4 = sb("lg4", [P, BT, E0])
        oh1 = sb("oh1", [P, BT, E0])
        mx = sb("mx", [P, BT])
        mn = sb("mn", [P, BT])
        ohb = sb("ohb", [P, BT, E0], BF16)
        ohT = sb("ohT", [E0, BLK], BF16)
        ohTf = sb("ohTf", [E0, BLK])
        tmp = sb("tmp", [P, 512])

        const_loaded = sem("const_loaded")
        weights_loaded = sem("weights_loaded")
        operands_set = sem("operands_set")
        consts_made = sem("consts_made")
        in_loaded = [sem("in_loaded0"), sem("in_loaded1")]
        q_stored = [sem("q_stored0"), sem("q_stored1")]
        k_stored = [sem("k_stored0"), sem("k_stored1")]
        qk_loaded = [sem("qk_loaded0"), sem("qk_loaded1")]
        rows_landed = [sem("rows_landed0"), sem("rows_landed1")]
        res_loaded = [sem("res_loaded0"), sem("res_loaded1")]
        out_stored = [sem("out_stored0"), sem("out_stored1")]
        s_filled = sem("s_filled")
        s_drained = sem("s_drained")
        e_filled = sem("e_filled")
        probs_ready = sem("probs_ready")
        av_filled = sem("av_filled")
        av_drained = sem("av_drained")
        misc_filled = sem("misc_filled")
        misc_drained = sem("misc_drained")
        q_ready = sem("q_ready")
        k_ready = sem("k_ready")
        q_split = sem("q_split")
        k_split = sem("k_split")
        max_split = sem("max_split")
        stats_ready = sem("stats_ready")
        rstd_ready = sem("rstd_ready")
        norm_ready = sem("norm_ready")
        fin_loaded = [sem("fin_loaded0"), sem("fin_loaded1")]
        f_loaded = [sem("f_loaded0"), sem("f_loaded1")]
        f_stats = sem("f_stats")
        f_rstd = sem("f_rstd")
        f_norm = sem("f_norm")
        gate_ready = sem("gate_ready")
        exp_in = sem("exp_in")
        exp_out = sem("exp_out")
        mask_filled = sem("mask_filled")
        hid_filled = sem("hid_filled")
        hid_ready = sem("hid_ready")
        gated_ready = sem("gated_ready")
        gated_used = sem("gated_used")
        y_filled = sem("y_filled")
        y_ready = sem("y_ready")

        plan = []
        misc_at = 0
        stored_at = 0
        fstat_at = fnorm_at = fload_at = fin_at = 0
        hid_at = mask_at = ga_at = gate_at = yb_at = 0
        order = ["norm0", "att0", "moe0", "att1", "att2", "ffn", "att3", "moe1"]
        atts = {a.name: a for a in ATTS}
        for name in order:
            ph = {"name": name, "misc": misc_at, "stored": stored_at}
            if name in atts:
                ph["att"] = atts[name]
                ph["segs"], post, misc_at = att_steps(atts[name], misc_at, True, post if name == "att2" else ())
                stored_at += 2 * 16 * B // 2
            else:
                if name != "norm0":
                    ph["before"], ph["post"] = plan[-1]["att"], post
                ph.update(fstat=fstat_at, fnorm=fnorm_at, fload=fload_at, fin=fin_at, hid=hid_at, mask=mask_at,
                          ga=ga_at, gate=gate_at, y=yb_at)
                misc_at += len(FF_ORDER[name])
                stored_at += 16 * NBLK // 2 * {"norm0": 1, "moe0": 3, "ffn": 3, "moe1": 1}[name]
                fload_at += 8 * NBLK // 2 * {"norm0": 1, "moe0": 2, "ffn": 4, "moe1": 4}[name]
                fin_at += 16 * NBLK // 2 // (1 + (name == "norm0"))
                fstat_at += NBLK * {"norm0": 1, "moe0": 1, "ffn": 3, "moe1": 0}[name]
                fnorm_at += NBLK * {"norm0": 1, "moe0": 1, "ffn": 1, "moe1": 0}[name]
                hid_at += NBLK * {"norm0": 0, "moe0": E0 * 4, "ffn": 4, "moe1": E1 * 3}[name]
                ga_at += NBLK * {"norm0": 0, "moe0": E0 * 4, "ffn": 0, "moe1": E1 * 3}[name]
                mask_at += NBLK * {"norm0": 0, "moe0": E0, "ffn": 0, "moe1": E1}[name]
                gate_at += NBLK * {"norm0": 0, "moe0": 1, "ffn": 0, "moe1": 1}[name]
                yb_at += NBLK * (name != "norm0")
            plan.append(ph)
        FF = {
            "norm0": dict(misc=1, loads=1, stats=1, norm=1, stores=1),
            "moe0": dict(misc=4, loads=1, stats=1, norm=1, stores=3, experts=E0, tiles=4, lag=4),
            "ffn": dict(misc=2, loads=2, stats=3, norm=1, stores=3, experts=1, tiles=4, lag=4),
            "moe1": dict(misc=3, loads=2, stats=0, norm=0, stores=1, experts=E1, tiles=3, lag=3),
        }
        for f in FF.values():
            f["hid"] = f.get("experts", 0) * f.get("tiles", 0)

        CONSTS = 16 * 6
        WEIGHTS = 16 * 10
        WEIGHTS0 = WEIGHTS + 16 * 8
        WEIGHTS2 = WEIGHTS0 + 16 * 5
        STORED0 = [next(p["stored"] for p in plan if p["name"] == a.name) for a in ATTS]

        FIRST_BLOCK = {a.n: plan[i - 1]["stored"] + 16 * FF[plan[i - 1]["name"]]["stores"] for a in ATTS
                       for i, p in enumerate(plan) if p["name"] == a.name and plan[i - 1]["name"] in FF}

        V_USE = {}
        for ph in plan:
            if "att" in ph:
                for iters, steps in ph["segs"]:
                    for st in steps:
                        if st[0] == "v":
                            V_USE[(ph["name"], st[1].k, st[1].m)] = st[3]

        def v_made(a, b):
            if (a.name, b.k, b.m) in V_USE:
                return V_USE[(a.name, b.k, b.m)] + 1
            base = V_USE[(a.name, 2, 2)]
            return Lin(base.k + (b.k - 2) * (base.m // 2) + 1, base.m if b.m else 0)

        def post_misc(ph, k):
            key = (("post", k), 0)
            return Lin(ph["misc"] + FF_ORDER[ph["name"]].index(key)) if key in FF_ORDER[ph["name"]] else None

        def post_step(step_fn, ph, k):
            kind, b, arg, use = ph["post"][k]
            step_fn(ph["before"], kind, b, arg, post_misc(ph, k), None)

        def tail_misc(ph, i):
            return FF_ORDER[ph["name"]].index(("nT", i))

        block = es.enter_context(nc.Block())

        def batch_no(a, b):
            return b + B * a.n

        def group_no(a, b, g):
            return (b + B * a.n) * NG + g

        def slot_no(a, b, s):
            return b * a.slots + (SLOT0[a.n] + s)

        def in_count(a, b):
            per = 16 if a.own_kv else 32
            return b.half() * per + (IN0[a.n] + per)

        def value(eng, c, j):
            return c.on(j) if j is None or c.m == 0 else eng.snap(c.on(j))

        def run_att(eng, ph, step_fn):
            for iters, steps in ph["segs"]:
                if iters:
                    with eng.Fori(0, iters) as j:
                        for st in steps:
                            step_fn(ph["att"], st[0], st[1], st[2], st[3], j)
                else:
                    for kind, b, arg, use in steps:
                        if kind == "before":
                            step_fn(ATTS[ph["att"].n - 1], arg[0], b, arg[1], use, None)
                        else:
                            step_fn(ph["att"], kind, b, arg, use, None)

        @block.sync
        def _(sp):
            n_const = [0]

            def const(dst, src):
                sp.dma_start(dst, src).then_inc(const_loaded, 16)
                n_const[0] += 1

            def weight(dst, src):
                sp.dma_start(dst, src).then_inc(weights_loaded, 16)

            count_regs = [sp.alloc_register(f"count{i}") for i in range(2)]

            def early(c, j, i):
                if j is None or c.m == 0:
                    return c.k
                sp.reg_mov(count_regs[i], c.on(j))
                return count_regs[i]

            def load_fin(name, i):
                sp.dma_start(fin[:, i % 2, :], feat[name][:, i * BLK:(i + 1) * BLK]).then_inc(fin_loaded[i % 2], 16)

            def load_block(ph, i):
                name, f = ph["name"], FF[ph["name"]]
                par = i % 2
                if i >= 2 and name != "norm0":
                    sp.wait_ge(out_stored[par], ph["stored"] + 16 * f["stores"] * (i // 2))
                blk = slice(i * BLK, (i + 1) * BLK)
                for dst, src in {"norm0": [(fres if i < 2 else fres2, "x")], "moe0": [(fres, "x1")], "ffn": [(fres, "y2"), (fres2, "x2")],
                                 "moe1": [(fres, "u"), (fres2, "x3")]}[name]:
                    landed = fin_loaded if name == "norm0" and i >= 2 else f_loaded
                    sp.dma_start(dst[:, par, :, :], rows[src][blk, :].rearrange("(t p) d -> p t d", p=P)) \
                        .then_inc(landed[par], 16)

            load_block(plan[0], 0)
            const(ident[:, :], dram["ident"])
            const(mask_f[:, :, :], dram["masks"])
            const(gates[:, 0:2], dram["g_xattn"].partition_broadcast(P))
            const(gates[:, 2:4], dram["g_ffn"].partition_broadcast(P))
            const(cols[:, :], dram["cols"])
            const(sel_f[:, :, :], dram["sel"])
            assert n_const[0] * 16 == CONSTS

            def store_block(ph, i):
                name, f, par = ph["name"], FF[ph["name"]], i % 2
                blk = slice(i * BLK, (i + 1) * BLK)
                if name != "norm0" and i + 2 < NBLK:
                    sp.wait_ge(y_filled, ph["y"] + i + 1)
                    load_fin(name, i + 2)
                if name == "ffn":
                    sp.wait_ge(f_stats, ph["fstat"] + 3 * i + 3)
                    store_rows(name, blk, par)
                if f["norm"]:
                    sp.wait_ge(misc_drained, ph["misc"] + tail_misc(ph, i) + 1)
                    nxt = {"norm0": "att0", "moe0": "att1", "ffn": "att3"}[name]
                    sp.dma_start(feat[nxt][:, blk], fT[:, :]).then_inc(out_stored[par], 16)
                else:
                    sp.wait_ge(y_ready, ph["y"] + i + 1)
                    sp.wait_ge(f_norm, 3 * NBLK + i + 1)
                if name != "ffn":
                    store_rows(name, blk, par)

            def store_rows(name, blk, par):
                for src, dst in {"norm0": [], "moe0": [(ft1, "x2"), (ft2, "z")], "ffn": [(ft2, "x3"), (ft3, "z4")],
                                 "moe1": [(ft1, "out")]}[name]:
                    sp.dma_start(rows[dst][blk, :].rearrange("(t p) d -> p t d", p=P), src[:, :, :]) \
                        .then_inc(out_stored[par], 16)

            def att_step(a, kind, b, arg, m, j):
                n = batch_no(a, b)
                par = b.odd()
                if kind == "weights":
                    if a.n == 0:
                        q = {0: 0, 5: 1, 6: 2, 7: 3}[b.k]
                        ex = slice(q * E0 // 4, (q + 1) * E0 // 4)
                        weight(w1_0[:, ex, :], dram["w1_0"][:, ex, :])
                        weight(w2_0[:, ex, :, :], dram["w2_0"][:, ex, :, :])
                    elif b.k == 0:
                        weight(fc1[:, :], dram["fc1"])
                        weight(fc2[:, :, :], dram["fc2"])
                    else:
                        dst, src = {5: (w1_1, "w1_1"), 6: (w3_1, "w3_1"), 7: (w2_1, "w2_1")}[b.k]
                        weight(dst, dram[src])
                elif kind == "loadin":
                    at = value(sp, b, j)
                    if a.name == "att2" and b.m == 0 and b.k <= 3:
                        count = STORED0[1] + 32 * ((b.k // 2 + 1) if b.k < 3 else B // 2)
                        sp.wait_ge(misc_filled, V_USE[("att1", B - 1, 0)].k + 1)
                        sp.wait_ge(out_stored[par], count)
                        if b.k == 3:
                            sp.wait_ge(out_stored[1 - par], count)
                    if a.name != "att2" and b.m == 0 and b.k <= 2:
                        if b.k == 0 or (b.k == 1 and a.own_kv):
                            sp.wait_ge(out_stored[0], FIRST_BLOCK[a.n])
                        else:
                            sp.wait_ge(out_stored[0], STORED0[a.n])
                            sp.wait_ge(out_stored[1], STORED0[a.n])
                    if b.m or b.k >= 2:
                        sp.wait_ge(misc_filled, v_made(a, b - 2).on(j))
                    src = feat[a.name].rearrange("p (b c) -> b p c", c=SQ)
                    sp.dma_start(inT[:, par, :], src[at]).then_inc(in_loaded[par], 16)
                    if not a.own_kv:
                        sp.dma_start(ctxT[:, par, :], dram["ctxT"][at]).then_inc(in_loaded[par], 16)
                elif kind == "qstore":
                    before = early(n.half() * 96, j, 0)
                    sp.wait_ge(q_split, (n + 1).on(j))
                    if n.m or n.k >= 2:
                        sp.wait_ge(qk_loaded[par], before)
                    sp.dma_start(q_scr[par].rearrange("t p c -> p t c"), qp[:, :, :]).then_inc(q_stored[par], 16)
                elif kind == "kstore":
                    sp.wait_ge(k_split, (n + 1).on(j))
                    dst = k_scr[par].rearrange("t p c -> p t c")[:, :, 0:a.keys]
                    sp.dma_start(dst[:, 0:3, :], kp[:, :, 0:a.keys]).then_inc(k_stored[par], 16)
                    sp.dma_start(dst[:, 3:5, :], kp[:, 0:2, 0:a.keys]).then_inc(k_stored[par], 16)
                elif kind == "loadqk":
                    stored_q = early((n.half() + 1) * 16, j, 0)
                    stored_k = early((n.half() + 1) * 32, j, 1)
                    if a.name == "att2" and b.m == 0 and b.k < 2:
                        sp.wait_ge(e_filled, SLOT0[a.n])
                    if b.m or b.k >= 2:
                        used = value(sp, slot_no(a, b - 1, 0), j)
                        sp.wait_ge(e_filled, used)
                    if a.n == 0 and b.m == 0 and b.k == 0:
                        sp.wait_ge(operands_set, 1)
                    sp.wait_ge(q_stored[par], stored_q)
                    q_src = q_scr[par].rearrange("t (d h) c -> (t d) h c", h=HEADS)
                    k_src = k_scr[par].rearrange("t (d h) c -> (t d) h c", h=HEADS)
                    w = PARTS * HD
                    for r in range(PARTS):
                        sp.dma_start(Qst[w * r:w * r + w, par, :, :], q_src).then_inc(qk_loaded[par], 16)
                    sp.wait_ge(k_stored[par], stored_k)
                    for r in range(PARTS):
                        sp.dma_start(Kst[w * r:w * r + w, par, :, 0:a.keys],
                                     k_src[HD * r:HD * r + w, :, 0:a.keys]).then_inc(qk_loaded[par], 16)
                elif kind == "maxT":
                    sp.wait_ge(misc_drained, (m + 1).on(j))
                    sp.dma_start(Qst[MROW:MROW + PARTS, par, GH * arg:GH * arg + GH, :], mrow[:, arg % 2, :]) \
                        .then_inc(rows_landed[arg % 2], 16)
                elif kind == "loadres":
                    src = rows[RES[a.name][0]].rearrange("(b t p) d -> b p t d", p=P, t=QT)
                    sp.dma_start(res[:, par, :, :], src[b.on(j)]).then_inc(res_loaded[par], 16)
                elif kind == "nT":
                    at = value(sp, b, j)
                    sp.wait_ge(misc_drained, (m + 1).on(j))
                    dst = rows[RES[a.name][1]].rearrange("(b t p) d -> b p t d", p=P, t=QT)
                    own = newres if a.tail != "affine" else normed
                    sp.dma_start(dst[at], own[:, par, :, :]).then_inc(out_stored[par], 16)
                    dst = feat[NEXT[a.name]].rearrange("p (b c) -> b p c", c=SQ)
                    sp.dma_start(dst[at], nT[:, :]).then_inc(out_stored[par], 16)

            for ph in plan:
                if "post" in ph:
                    first = STORED0[ph["before"].n]
                    sp.wait_ge(out_stored[0], first + 64)
                    sp.wait_ge(out_stored[1], first + 64)
                    load_fin(ph["name"], 0)
                    load_fin(ph["name"], 1)
                    for k, st in enumerate(ph["post"]):
                        att_step(ph["before"], st[0], st[1], st[2], post_misc(ph, k), None)
                if ph["stored"] and "att" not in ph:
                    sp.wait_ge(out_stored[0], ph["stored"])
                    sp.wait_ge(out_stored[1], ph["stored"])
                if ph["name"] == "norm0":
                    for i in range(1, NBLK):
                        load_block(ph, i)
                    weight(wts[:, :, :], dram["wts"].rearrange("w p d -> p w d"))
                    weight(vecs[:, :, :].rearrange("p a b -> p (a b)"),
                           dram["vecs"].rearrange("a b -> (a b)").partition_broadcast(P))
                    weight(ropes[:, :, :], dram["ropes"])
                    weight(gw0[:, :], dram["gw0"])
                    weight(gb0[:, :], dram["gb0"].partition_broadcast(P))
                    weight(iota[:, :], dram["iota"].partition_broadcast(P))
                    weight(b1_0[:, :, :], dram["b1_0"])
                    weight(b2_0[:, :], dram["b2_0"])
                    weight(fc1b[:, :], dram["fc1b"])
                    weight(gw1[:, :], dram["gw1"])
                    for i in range(NBLK):
                        store_block(ph, i)
                elif "att" in ph:
                    run_att(sp, ph, att_step)
                else:
                    load_block(ph, 0)
                    load_block(ph, 1)
                    for i in range(NBLK):
                        store_block(ph, i)
                        if i + 2 < NBLK:
                            load_block(ph, i + 2)
            sp.wait_ge(out_stored[0], plan[-1]["stored"] + 16 * NBLK // 2)
            sp.wait_ge(out_stored[1], plan[-1]["stored"] + 16 * NBLK // 2)

        @block.gpsimd
        def _(po):
            for tile, value in ((nhalf[:, :], -0.5), (epss[:, 0, :], EPS), (epss[:, 1, :], EPS_RMS), (zero8, 0.0),
                                (Kst[64:P, :, :, :].bitcast(F32), 0.0), (Qst[64:P, :, :, :].bitcast(F32), 0.0)):
                po.memset(tile, value)
                po.drain()

            def ones_rows():
                po.drain()
                po.memset(Kst[MROW:P, :, :, :].bitcast(F32), TWO_ONES).then_inc(operands_set, 1)

            def split(src, parts, r, c0, c1, sem_in, count, j):
                po.drain()
                po.wait_ge(sem_in, count)
                po.tensor_tensor(r[:, c0:c1], src[:, c0:c1], parts[:, 0, c0:c1], ALU.subtract)
                po.drain()
                po.tensor_copy(parts[:, 1, c0:c1], r[:, c0:c1])
                po.drain()
                return po.tensor_tensor(parts[:, 2, c0:c1], r[:, c0:c1], parts[:, 1, c0:c1], ALU.subtract)

            def att_step(a, kind, b, arg, m, j):
                n = batch_no(a, b)
                if kind == "qsplit":
                    split(qf, qp, rq, 0, SQ, q_ready, (n + 1).on(j), j).then_inc(q_split, 1)
                elif kind == "ksplit":
                    last = split(kf, kp, rk, SQ * arg, SQ * arg + SQ, k_ready, (n + 1).on(j), j)
                    if arg == a.kt // 2 - 1:
                        last.then_inc(k_split, 1)
                elif kind == "maxsplit":
                    g = group_no(a, b, arg)
                    po.drain()
                    po.wait_ge(s_drained, (slot_no(a, b, (arg + 1) * a.gs) * 2).on(j))
                    if g.m or g.k >= 4:
                        po.wait_ge(rows_landed[arg % 2], (g.half() * 16 - 16).on(j))
                    src = nmax[:, arg, :, :]
                    r3 = mres[:, 0, :].rearrange("p (a b) -> p a b", a=QT)
                    r4 = mres[:, 1, :].rearrange("p (a b) -> p a b", a=QT)
                    dst = mparts[:, arg, :, :, :]
                    po.tensor_tensor(dst[:, :, 0, :], src, zero8, ALU.add)
                    po.drain()
                    po.tensor_tensor(r3, src, dst[:, :, 0, :], ALU.subtract)
                    po.drain()
                    po.tensor_copy(dst[:, :, 1, :], r3)
                    po.drain()
                    po.tensor_tensor(dst[:, :, 2, :], r3, dst[:, :, 1, :], ALU.subtract).then_inc(max_split, 1)
                elif kind in ("resid", "proj"):
                    po.drain()
                    po.wait_ge(stats_ready, (n + 1).on(j))
                    rsqrt(QT, 2 if a.tail == "rms" else 1).then_inc(rstd_ready, 1)

            def rsqrt(t, how):
                if how == 2:
                    po.tensor_tensor(rin[:, 0:t], mv[:, 0:t, 0], mv[:, 0:t, 0], ALU.mult)
                    po.drain()
                    po.tensor_tensor(rin[:, 0:t], rin[:, 0:t], mv[:, 0:t, 1], ALU.add)
                    po.drain()
                    po.tensor_tensor(rin[:, 0:t], rin[:, 0:t], epss[:, 1, 0:t], ALU.add)
                else:
                    po.tensor_tensor(rin[:, 0:t], mv[:, 0:t, 1], epss[:, 0, 0:t], ALU.add)
                po.drain()
                return po.tensor_tensor(rstd[:, 0:t], rin[:, 0:t], nhalf[:, 0:t], ALU.pow)

            for ph in plan:
                if "att" in ph:
                    run_att(po, ph, att_step)
                else:
                    f = FF[ph["name"]]
                    for st in ph.get("post", ()):
                        att_step(ph["before"], st[0], st[1], st[2], None, None)
                    for i in range(NBLK):
                        for s in range(f["stats"]):
                            po.drain()
                            po.wait_ge(f_stats, ph["fstat"] + i * f["stats"] + s + 1)
                            rms = ph["name"] == "ffn" and s == 2
                            rsqrt(BT, 2 if rms else 1).then_inc(f_rstd, 1)
                    if ph["name"] == "norm0":
                        ones_rows()

        @block.scalar
        def _(act):
            act.wait_ge(const_loaded, CONSTS)
            act.activation(tg[:, :], gates[:, :], ACT.Tanh)
            act.activation(maskb[:, :, :], mask_f[:, :, :], ACT.Copy)
            act.activation(sel_b[:, :, :], sel_f[:, :, :], ACT.Copy)
            act.activation(identb[:, :], ident[:, :], ACT.Copy)
            act.activation(qbias[:, :], cols[:, :], ACT.Copy, scale=SCALE).then_inc(consts_made, 1)
            act.wait_ge(consts_made, 1)

            def att_step(a, kind, b, arg, m, j):
                n = batch_no(a, b)
                par = b.odd()
                if kind == "E":
                    c = slot_no(a, b, arg)
                    act.wait_ge(e_filled, (c + 1).on(j))
                    back = arg - RING
                    if b.m or b.k > 0 or back >= 0:
                        gb = group_no(a, b, 0) + back // a.gs
                        act.wait_ge(av_filled, (gb + 1).on(j))
                    dst, src = prob[:, arg % RING, :], e_ps[:, arg % 2, :]
                    if a.rope:
                        dst = dst.rearrange("p (h c) -> p h c", h=a.hps)[:, :, 0:SQ + P]
                        src = src.rearrange("p (h c) -> p h c", h=a.hps)[:, :, 0:SQ + P]
                    act.activation(dst, src, ACT.Exp).then_inc(probs_ready, 1)
                elif kind == "AV" and arg[1] == a.gs - 1:
                    act.wait_ge(av_filled, (group_no(a, b, arg[0]) + 1).on(j))
                    act.activation(OT[:, par, arg[0], :], av_ps[:, 0:SQ], ACT.Copy).then_inc(av_drained, 1)
                elif kind == "q" and not a.rope:
                    act.wait_ge(misc_filled, (m + 1).on(j))
                    if n.m or n.k >= 1:
                        act.wait_ge(q_stored[1 - par], ((n + 1).half() * 16).on(j))
                    c = CI[a.name + "_q"]
                    act.activation(qf[:, :], misc[:, 0:SQ], ACT.Identity, bias=qbias[:, c:c + 1], scale=SCALE)
                    act.activation(qp[:, 0, :], misc[:, 0:SQ], ACT.Identity, bias=qbias[:, c:c + 1], scale=SCALE) \
                        .then_inc(q_ready, 1)
                    act.wait_ge(q_ready, (n + 1).on(j))
                    act.sem_inc(misc_drained, 1)
                elif kind == "k" and not a.rope:
                    act.wait_ge(misc_filled, (m + 1).on(j))
                    if n.m or n.k >= 1:
                        act.wait_ge(k_stored[1 - par], ((n + 1).half() * 32).on(j))
                    c = CI[a.name + "_k"]
                    act.activation(kf[:, 0:a.keys], misc[:, 0:a.keys], ACT.Identity, bias=cols[:, c:c + 1])
                    act.activation(kp[:, 0, 0:a.keys], misc[:, 0:a.keys], ACT.Identity, bias=cols[:, c:c + 1]) \
                        .then_inc(k_ready, 1)
                    act.wait_ge(k_ready, (n + 1).on(j))
                    act.sem_inc(misc_drained, 1)
                elif kind == "maxT":
                    gn = group_no(a, b, arg)
                    act.wait_ge(misc_filled, (m + 1).on(j))
                    if gn.m or gn.k >= 2:
                        act.wait_ge(rows_landed[arg % 2], (gn.half() * 16).on(j))
                    act.activation(mrow[:, arg % 2, :], misc[0:PARTS * GH, :].bitcast(BF16)[:, 0:SQ], ACT.Copy) \
                        .then_inc(misc_drained, 1)
                elif kind == "aT":
                    act.wait_ge(misc_filled, (m + 1).on(j))
                    act.activation(aT[:, :], misc[:, 0:SQ], ACT.Copy).then_inc(misc_drained, 1)
                elif kind == "nT":
                    act.wait_ge(misc_filled, (m + 1).on(j))
                    act.wait_ge(out_stored[1 - par], ((b + 1).half() * 32 + STORED0[a.n]).on(j))
                    act.activation(nT[:, :], misc[:, 0:SQ], ACT.Copy).then_inc(misc_drained, 1)

            def ff_block(ph):
                name, f = ph["name"], FF[ph["name"]]
                for kind, i in FF_STEPS[name]:
                    if kind[0] == "post":
                        post_step(att_step, ph, kind[1])
                    elif kind == "nT":
                        act.wait_ge(misc_filled, ph["misc"] + FF_ORDER[name].index((kind, i)) + 1)
                        act.wait_ge(out_stored[1 - i % 2], ph["stored"] + 16 * f["stores"] * ((i + 1) // 2))
                        act.activation(fT[:, :], misc[:, :], ACT.Copy).then_inc(misc_drained, 1)
                    elif kind == "choose" and name == "moe1":
                        act.wait_ge(exp_in, i + 1)
                        act.activation(lg3[:, :, 0:E1], lg2[:, :, 0:E1], ACT.Exp).then_inc(exp_out, 1)
                    elif kind == "y":
                        act.wait_ge(y_filled, ph["y"] + i + 1)
                        if i:
                            act.wait_ge(misc_filled, ph["misc"] + FF_ORDER[name].index(("back", i - 1)) + 1)
                        bias = cols[:, CI["fc2_b"]:CI["fc2_b"] + 1] if name == "ffn" else 0.0
                        act.activation(ysb[:, :], av_ps[:, :], ACT.Identity, bias=bias).then_inc(y_ready, 1)
                    elif isinstance(kind, tuple) and kind[0] == "h":
                        e, t = kind[1:]
                        c = i * f["hid"] + e * f["tiles"] + t
                        act.wait_ge(hid_filled, ph["hid"] + c + 1)
                        if name == "ffn":
                            if c >= 8:
                                act.wait_ge(gated_used, ph["hid"] + c - 7)
                            act.activation(hid[:, c % 8, :], hid_ps[:, c % 4, :], ACT.Relu,
                                           bias=fc1b[:, t:t + 1]).then_inc(hid_ready, 1)
                        elif name == "moe0":
                            if c >= 8:
                                act.wait_ge(gated_ready, c - 7)
                            act.activation(hid[:, c % 8, :], hid_ps[:, c % 4, :], ACT.Relu,
                                           bias=b1_0[:, e, t:t + 1]).then_inc(hid_ready, 1)
                        else:
                            if c >= 8:
                                act.wait_ge(gated_ready, NBLK * E0 * 4 + c - 7)
                            act.activation(hid[:, c % 8, :], hid_ps[:, 2 * (c % 2), :], ACT.Silu) \
                                .then_inc(hid_ready, 1)

            for n, ph in enumerate(plan):
                if n == 1:
                    act.wait_ge(weights_loaded, WEIGHTS)
                if ph["name"] == "att1":
                    act.wait_ge(out_stored[0], ph["stored"])
                    act.wait_ge(out_stored[1], ph["stored"])
                if "att" in ph:
                    run_att(act, ph, att_step)
                else:
                    ff_block(ph)

        @block.vector
        def _(ve):
            ve.memset(Vx[:, :, :, :, :], 0.0)
            ve.drain()
            ve.memset(Vx[:, :, :, :, HD:HD + 1], 1.0)
            ve.wait_ge(consts_made, 1)

            def stats_of(src, t):
                ve.drain()
                for i in range(t):
                    ve.bn_stats(stats[:, i, :], src[:, i, :])
                ve.drain()
                for i in range(t):
                    last = ve.bn_aggr(mv[:, i, :], stats[:, i, :])
                return last

            def apply_norm(dst, src, t, rms=False):
                for i in range(t):
                    if rms:
                        last = ve.tensor_scalar(dst[:, i, :], src[:, i, :], rstd[:, i:i + 1], None, ALU.mult)
                    else:
                        last = ve.tensor_scalar(dst[:, i, :], src[:, i, :], mv[:, i, 0:1], rstd[:, i:i + 1],
                                                ALU.subtract, ALU.mult)
                return last

            def over(v, t):
                return vecs[:, VI[v], :].unsqueeze(1).to_broadcast([P, t, D])

            def att_step(a, kind, b, arg, m, j):
                n = batch_no(a, b)
                par = b.odd()
                if kind == "S":
                    s, u = arg
                    c = slot_no(a, b, s) * 2 + u
                    ve.wait_ge(s_filled, (c + 1).on(j))
                    g = s // a.gs
                    gn = group_no(a, b, g)
                    if s % a.gs == 0 and u == 0 and (gn.m or gn.k >= 4):
                        ve.wait_ge(max_split, (gn - 3).on(j))
                    if a.kt == 4:
                        h = s
                        ve.tensor_reduce(nmax[:, g, u, h % GH:h % GH + 1], s_ps[:, u, :], AX.X, ALU.max,
                                         negate=True).then_inc(s_drained, 1)
                    else:
                        h = 2 * s + u
                        ve.tensor_reduce(nmax[:, g, :, h % GH:h % GH + 1],
                                         s_ps[:, u, :].rearrange("p (t k) -> p t k", t=QT), AX.X, ALU.max,
                                         negate=True).then_inc(s_drained, 1)
                elif kind in ("q", "k") and a.rope:
                    first = 0 if kind == "q" else 2
                    dst, parts, ready = (qf, qp, q_ready) if kind == "q" else (kf, kp, k_ready)
                    ve.drain()
                    ve.wait_ge(misc_filled, (m + 1).on(j))
                    stored, per = (q_stored, 16) if kind == "q" else (k_stored, 32)
                    ve.wait_ge(stored[1 - par], ((n + 1).half() * per).on(j))
                    ve.tensor_tensor(rt[:, 0, :], misc[:, 0:SQ], ropes[:, first, :], ALU.mult)
                    ve.tensor_tensor(rt[:, 1, :], misc[:, SQ:2 * SQ], ropes[:, first + 1, :], ALU.mult) \
                        .then_inc(misc_drained, 1)
                    ve.drain()
                    ve.tensor_tensor(dst[:, 0:SQ], rt[:, 0, :], rt[:, 1, :], ALU.add)
                    ve.drain()
                    ve.tensor_copy(parts[:, 0, 0:SQ], dst[:, 0:SQ]).then_inc(ready, 1)
                elif kind == "v":
                    ve.wait_ge(misc_filled, (m + 1).on(j))
                    if n.m or n.k >= 2:
                        ve.wait_ge(av_filled, group_no(a, b - 1, 0).on(j))
                    dst = Vx[:, par, 0:a.kt, :, 0:HD]
                    src = misc[:, 0:a.kt * D].rearrange("p (t h d) -> p t h d", t=a.kt, h=HEADS)
                    for t in range(a.kt):
                        if a.rope:
                            last = ve.tensor_copy(dst[:, t], src[:, t])
                        else:
                            bv = vecs[:, VI[a.name + "_bv"], :].rearrange("p (h d) -> p h d", h=HEADS)
                            last = ve.tensor_tensor(dst[:, t], src[:, t], bv, ALU.add)
                    last.then_inc(misc_drained, 1)
                elif kind == "ctx":
                    ve.drain()
                    ve.wait_ge(misc_filled, (m + 1).on(j))
                    src = misc[:, :].rearrange("p (h c) -> p h c", c=VW)
                    ve.reciprocal(rden[:, :].unsqueeze(2), src[:, :, HD:HD + 1])
                    ve.drain()
                    ve.tensor_tensor(att[:, arg, :].rearrange("p (h d) -> p h d", h=HEADS), src[:, :, 0:HD],
                                     rden[:, :].unsqueeze(2).to_broadcast([P, HEADS, HD]), ALU.mult) \
                        .then_inc(misc_drained, 1)
                elif kind in ("resid", "proj"):
                    ve.drain()
                    ve.wait_ge(res_loaded[par], ((n.half() + 1) * 16).on(j))
                    ve.wait_ge(out_stored[par], (b.half() * 32 + STORED0[a.n]).on(j))
                    new, old = newres[:, par, :, :], res[:, par, :, :]
                    if kind == "resid":
                        ve.tensor_tensor(new, old, att[:, :, :], ALU.add)
                    else:
                        ve.wait_ge(misc_filled, (m + 1).on(j))
                        src = misc[:, 0:SQ].rearrange("p (t d) -> p t d", t=QT)
                        if a.tail == "gate":
                            t3 = tmp[:, 0:SQ].rearrange("p (t d) -> p t d", t=QT)
                            ve.tensor_tensor(t3, src, over("att0_bo", QT), ALU.add).then_inc(misc_drained, 1)
                            ve.drain()
                            ve.scalar_tensor_tensor(out=new, in0=t3, scalar=tg[:, GI["att0"]:GI["att0"] + 1],
                                                    in1=old, op0=ALU.mult, op1=ALU.add)
                        else:
                            ve.tensor_tensor(new, src, old, ALU.add).then_inc(misc_drained, 1)
                    stats_of(newres[:, par, :, :], QT).then_inc(stats_ready, 1)
                elif kind == "apply":
                    ve.drain()
                    ve.wait_ge(rstd_ready, (n + 1).on(j))
                    dst = normed[:, par, :, :]
                    if a.tail == "gate":
                        apply_norm(dst, newres[:, par, :, :], QT).then_inc(norm_ready, 1)
                    else:
                        t3 = tmp[:, 0:SQ].rearrange("p (t d) -> p t d", t=QT)
                        t4 = tmp[:, SQ:2 * SQ].rearrange("p (t d) -> p t d", t=QT)
                        apply_norm(t3, newres[:, par, :, :], QT, rms=a.tail == "rms")
                        ve.drain()
                        if a.tail == "rms":
                            ve.tensor_tensor(dst, t3, over("att3_g", QT), ALU.mult).then_inc(norm_ready, 1)
                        else:
                            ve.tensor_tensor(t4, t3, over(a.name + "_g", QT), ALU.mult)
                            ve.drain()
                            ve.tensor_tensor(dst, t4, over(a.name + "_b", QT), ALU.add).then_inc(norm_ready, 1)

            def one_hot(dst, src, e, top):
                bc = [P, BT, e]
                io = iota[:, E0 - e:E0].unsqueeze(1).to_broadcast(bc)
                ve.tensor_reduce(top[:, :], src, AX.X, ALU.max)
                ve.drain()
                ve.tensor_tensor(lg4[:, :, 0:e], src, top[:, :].unsqueeze(2).to_broadcast(bc), ALU.is_equal)
                ve.drain()
                ve.tensor_tensor(lg4[:, :, 0:e], lg4[:, :, 0:e], io, ALU.mult)
                ve.drain()
                ve.tensor_reduce(mn[:, :], lg4[:, :, 0:e], AX.X, ALU.min)
                ve.drain()
                ve.tensor_tensor(dst, mn[:, :].unsqueeze(2).to_broadcast(bc), io, ALU.is_equal)
                ve.drain()

            def ff_block(ph):
                name, f = ph["name"], FF[ph["name"]]
                for kind, i in FF_STEPS[name]:
                    if kind[0] == "post":
                        post_step(att_step, ph, kind[1])
                        continue
                    par = i % 2
                    idx = ph["misc"] + (FF_ORDER[name].index((kind, i)) if (kind, i) in FF_ORDER[name] else 0)
                    loaded = ph["fload"] + 16 * f["loads"] * (i // 2 + 1)
                    stored = ph["stored"] + 16 * f["stores"] * ((i + 1) // 2)
                    if kind == "norm":
                        ve.wait_ge((f_loaded if i < 2 else fin_loaded)[par], 16)
                        x = (fres if i < 2 else fres2)[:, par, :, :]
                        stats_of(x, BT).then_inc(f_stats, 1)
                        ve.wait_ge(f_rstd, ph["fstat"] + i + 1)
                        if i:
                            ve.wait_ge(misc_filled, ph["misc"] + i)
                        apply_norm(ft3, x, BT).then_inc(f_norm, 1)
                    elif kind == "gate":
                        ve.wait_ge(misc_filled, idx + 1)
                        e = f["experts"]
                        src = misc[:, 0:BT * e].rearrange("p (t e) -> p t e", e=e)
                        ve.drain()
                        if name == "moe0":
                            ve.tensor_tensor(lg[:, :, :], src, gb0[:, :].unsqueeze(1).to_broadcast([P, BT, E0]),
                                             ALU.add).then_inc(misc_drained, 1)
                        else:
                            ve.tensor_copy(lg[:, :, 0:E1], src).then_inc(misc_drained, 1)
                    elif kind == "choose":
                        e = f["experts"]
                        ve.drain()
                        if name == "moe0":
                            one_hot(oh1[:, :, :], lg[:, :, :], E0, mx)
                            ve.tensor_copy(ohb[:, :, :], oh1[:, :, :]).then_inc(gate_ready, 1)
                        else:
                            bc = [P, BT, E1]
                            l, l2, l3 = lg[:, :, 0:E1], lg2[:, :, 0:E1], lg3[:, :, 0:E1]
                            wide = lambda v: v[:, :].unsqueeze(2).to_broadcast(bc)
                            ve.tensor_reduce(mx[:, :], l, AX.X, ALU.max)
                            ve.drain()
                            ve.tensor_tensor(l2, l, wide(mx), ALU.subtract).then_inc(exp_in, 1)
                            ve.wait_ge(exp_out, i + 1)
                            ve.tensor_reduce(mx[:, :], l3, AX.X, ALU.add)
                            ve.drain()
                            ve.reciprocal(mn[:, :], mx[:, :])
                            ve.drain()
                            ve.tensor_tensor(l, l3, wide(mn), ALU.mult)
                            ve.drain()
                            one_hot(oh1[:, :, 0:E1], l, E1, mx)
                            ve.scalar_tensor_tensor(out=l2, in0=oh1[:, :, 0:E1], scalar=-2.0, in1=l, op0=ALU.mult,
                                                    op1=ALU.add)
                            ve.drain()
                            one_hot(l3, l2, E1, mx)
                            ve.tensor_tensor(l2, oh1[:, :, 0:E1], l3, ALU.add)
                            ve.drain()
                            ve.tensor_tensor(l3, l2, l, ALU.mult)
                            ve.drain()
                            ve.tensor_reduce(mx[:, :], l3, AX.X, ALU.add)
                            ve.drain()
                            ve.reciprocal(mn[:, :], mx[:, :])
                            ve.drain()
                            ve.tensor_tensor(oh1[:, :, 0:E1], l3, wide(mn), ALU.mult).then_inc(gate_ready, 1)
                    elif kind == "spread":
                        ve.wait_ge(misc_filled, idx + 1)
                        if i:
                            ve.wait_ge(mask_filled, ph["mask"] + i * f["experts"])
                        if name == "moe0":
                            src = misc[0:E0, :].bitcast(BF16)[:, 0:BLK]
                            ve.tensor_copy(ohT[:, :], src)
                            ve.tensor_copy(ohTf[:, :], src).then_inc(misc_drained, 1)
                        else:
                            ve.tensor_copy(ohTf[0:E1, :], misc[0:E1, :]).then_inc(misc_drained, 1)
                    elif isinstance(kind, tuple) and kind[0] == "h" and name != "ffn":
                        e, t = kind[1:]
                        c = i * f["hid"] + e * f["tiles"] + t
                        ve.wait_ge(hid_ready, ph["hid"] + c + 1)
                        if c >= 8:
                            ve.wait_ge(gated_used, ph["hid"] + c - 7)
                        mk = i * f["experts"] + e
                        ve.wait_ge(mask_filled, ph["mask"] + mk + 1)
                        if name == "moe0":
                            ve.tensor_tensor(gated[:, c % 8, :], hid[:, c % 8, :], s_ps[:, mk % 2, :], ALU.mult) \
                                .then_inc(gated_ready, 1)
                        else:
                            ve.wait_ge(hid_filled, ph["hid"] + c + 1)
                            ve.drain()
                            ve.tensor_tensor(tmp[:, :], hid[:, c % 8, :], hid_ps[:, 2 * (c % 2) + 1, :], ALU.mult)
                            ve.drain()
                            ve.tensor_tensor(gated[:, c % 8, :], tmp[:, :], s_ps[:, mk % 2, :], ALU.mult) \
                                .then_inc(gated_ready, 1)
                    elif kind == "back":
                        ve.wait_ge(misc_filled, idx + 1)
                        ve.wait_ge(f_loaded[par], loaded)
                        ve.wait_ge(out_stored[1 - par], stored)
                        src = misc[:, :].rearrange("p (t d) -> p t d", t=BT)
                        g = tg[:, GI[name]:GI[name] + 1]
                        ve.drain()
                        if name == "moe0":
                            ve.scalar_tensor_tensor(out=ft1[:, :, :], in0=src, scalar=g, in1=fres[:, par, :, :],
                                                    op0=ALU.mult, op1=ALU.add).then_inc(misc_drained, 1)
                            stats_of(ft1, BT).then_inc(f_stats, 1)
                        elif name == "ffn":
                            ve.tensor_tensor(ft1[:, :, :], src, fres[:, par, :, :], ALU.add).then_inc(misc_drained, 1)
                            stats_of(ft1, BT).then_inc(f_stats, 1)
                        else:
                            ve.tensor_tensor(ft2[:, :, :], src, fres[:, par, :, :], ALU.add).then_inc(misc_drained, 1)
                            ve.drain()
                            ve.scalar_tensor_tensor(out=ft1[:, :, :], in0=ft2[:, :, :], scalar=g,
                                                    in1=fres2[:, par, :, :], op0=ALU.mult, op1=ALU.add) \
                                .then_inc(f_norm, 1)
                    elif kind == "tail2":
                        ve.wait_ge(f_rstd, ph["fstat"] + i * f["stats"] + 1)
                        if name == "moe0":
                            if i:
                                ve.wait_ge(misc_filled, ph["misc"] + FF_ORDER[name].index(("nT", i - 1)) + 1)
                            apply_norm(ft2, ft1, BT).then_inc(f_norm, 1)
                        else:
                            t3 = tmp[:, :].rearrange("p (t d) -> p t d", t=BT)
                            apply_norm(ft2, ft1, BT)
                            ve.drain()
                            ve.tensor_tensor(ft3[:, :, :], ft2[:, :, :], over("ffn_g", BT), ALU.mult)
                            ve.drain()
                            ve.tensor_tensor(t3, ft3[:, :, :], over("ffn_b", BT), ALU.add)
                            ve.drain()
                            ve.scalar_tensor_tensor(out=ft2[:, :, :], in0=t3, scalar=tg[:, GI["ffn"]:GI["ffn"] + 1],
                                                    in1=fres2[:, par, :, :], op0=ALU.mult, op1=ALU.add)
                            stats_of(ft2, BT).then_inc(f_stats, 1)
                    elif kind == "tail3":
                        ve.wait_ge(f_rstd, ph["fstat"] + i * f["stats"] + 2)
                        apply_norm(ft3, ft2, BT)
                        stats_of(ft3, BT).then_inc(f_stats, 1)
                    elif kind == "tail4":
                        ve.wait_ge(f_rstd, ph["fstat"] + i * f["stats"] + 3)
                        t3 = tmp[:, :].rearrange("p (t d) -> p t d", t=BT)
                        apply_norm(tmp[:, :].rearrange("p (t d) -> p t d", t=BT), ft3, BT, rms=True)
                        ve.drain()
                        ve.tensor_tensor(ft1[:, :, :], t3, over("g1", BT), ALU.mult).then_inc(f_norm, 1)

            for ph in plan:
                if ph["name"] == "att3":
                    ve.wait_ge(out_stored[0], ph["stored"])
                    ve.wait_ge(out_stored[1], ph["stored"])
                if "att" in ph:
                    run_att(ve, ph, att_step)
                else:
                    ff_block(ph)

        @block.tensor
        def _(pe):
            pe.wait_ge(consts_made, 1)

            def take_misc(m, j):
                if m.m or m.k > 0:
                    pe.wait_ge(misc_drained, m.on(j))

            def att_step(a, kind, b, arg, m, j):
                n = batch_no(a, b)
                par = b.odd()
                kv = inT if a.own_kv else ctxT
                if m is not None:
                    take_misc(m, j)
                if kind == "S":
                    s, u = arg
                    c = slot_no(a, b, s) * 2 + u
                    if s == 0 and u == 0:
                        pe.wait_ge(qk_loaded[par], ((n.half() + 1) * 96).on(j))
                    if c.m or c.k >= 2:
                        pe.wait_ge(s_drained, (c - 1).on(j))
                    if a.kt == 4:
                        last = pe.matmul(s_ps[:, u, :], Qst[0:ROWS, par, s, u * P:u * P + P],
                                         Kst[0:ROWS, par, s, :], start=True, stop=True)
                    else:
                        h = 2 * s + u
                        for t in range(QT):
                            out = s_ps[:, u, t * SQ:t * SQ + SQ]
                            last = pe.matmul(out, Qst[0:ROWS, par, h, t * P:t * P + P],
                                             Kst[0:ROWS, par, h, 0:SQ], start=True, stop=not a.rope)
                            if a.rope:
                                o = s_ps[:, u, t * SQ:t * SQ + SQ]
                                if t == 0:
                                    last = pe.matmul(o[:, 0:P], identb[:, :], maskb[:, 0, :], start=False, stop=False)
                                    last = pe.matmul(o[:, P:SQ], identb[:, :], maskb[:, 2, :], start=False, stop=True)
                                else:
                                    last = pe.matmul(o[:, P:SQ], identb[:, :], maskb[:, 0, :], start=False, stop=True)
                    last.then_inc(s_filled, 1)
                elif kind == "E":
                    c = slot_no(a, b, arg)
                    if arg % a.gs == 0:
                        g = group_no(a, b, arg // a.gs)
                        pe.wait_ge(rows_landed[(arg // a.gs) % 2], (g.half() * 16 + 16).on(j))
                    if c.m or c.k >= 2:
                        pe.wait_ge(probs_ready, (c - 1).on(j))
                    for hh in range(a.hps):
                        h = arg * a.hps + hh
                        for t in range(a.kt):
                            col = (hh * a.kt + t) * SQ
                            o = e_ps[:, arg % 2, col:col + SQ]
                            if a.rope and t == 1:
                                o = e_ps[:, arg % 2, col:col + P]
                                pe.matmul(o, Kst[0:KROWS, par, h, P:SQ], Qst[0:KROWS, par, h, P:SQ], start=True,
                                          stop=False)
                                last = pe.matmul(o, identb[:, :], maskb[:, 1, :], start=False, stop=True)
                                continue
                            last = pe.matmul(o, Kst[0:KROWS, par, h, t * P:t * P + P], Qst[0:KROWS, par, h, :],
                                             start=True, stop=not a.rope)
                            if a.rope:
                                last = pe.matmul(o[:, 0:P], identb[:, :], maskb[:, 1, :], start=False, stop=True)
                    last.then_inc(e_filled, 1)
                elif kind == "AV":
                    g, t0 = arg
                    gn = group_no(a, b, g)
                    if t0 == 0:
                        pe.wait_ge(probs_ready, (slot_no(a, b, (g + 1) * a.gs)).on(j))
                        if gn.m or gn.k >= 1:
                            pe.wait_ge(av_drained, gn.on(j))
                    for t in range(t0 * a.kt // a.gs, (t0 + 1) * a.kt // a.gs):
                        for hh in range(GH):
                            h = GH * g + hh
                            slot, off = h // a.hps, (h % a.hps) * a.kt + t
                            w = P if a.rope and t == 1 else SQ
                            last = pe.matmul(av_ps[VW * hh:VW * hh + VW, SQ - w:SQ], Vx[:, par, t, h, :],
                                             prob[:, slot % RING, off * SQ:off * SQ + w],
                                             start=(t == 0), stop=(t == a.kt - 1))
                    if t0 == a.gs - 1:
                        last.then_inc(av_filled, 1)
                elif kind in ("q", "k"):
                    if kind == "q":
                        pe.wait_ge(in_loaded[par], in_count(a, b).on(j))
                        src, w = inT[:, par, :], SQ
                    else:
                        src, w = kv[:, par, 0:a.keys], a.keys
                    last = pe.matmul(misc[:, 0:w], wts[:, WI[f"{a.name}_{kind}"], :], src, start=True, stop=True)
                    if a.rope:
                        last = pe.matmul(misc[:, w:2 * w], wts[:, WI[f"{a.name}_{kind}s"], :], src, start=True,
                                         stop=True)
                    last.then_inc(misc_filled, 1)
                elif kind == "v":
                    for t in range(a.kt):
                        last = pe.matmul(misc[:, t * D:t * D + D], kv[:, par, t * P:t * P + P],
                                         wts[:, WI[a.name + "_v"], :], start=True, stop=True)
                    last.then_inc(misc_filled, 1)
                elif kind == "maxT":
                    pe.wait_ge(max_split, (group_no(a, b, arg) + 1).on(j))
                    for t in range(QT):
                        last = pe.transpose(misc[0:PARTS * GH, :].bitcast(BF16)[:, t * P:t * P + P],
                                            mparts[:, arg, t, :, :].rearrange("p a b -> p (a b)"), identb[:, :])
                    last.then_inc(misc_filled, 1)
                elif kind == "ctx":
                    if arg == 0:
                        pe.wait_ge(av_drained, (group_no(a, b, NG - 1) + 1).on(j))
                    for g in range(NG):
                        last = pe.transpose(misc[:, g * P:g * P + P], OT[:, par, g, arg * P:arg * P + P], ident[:, :])
                    last.then_inc(misc_filled, 1)
                elif kind == "aT":
                    for t in range(QT):
                        last = pe.transpose(misc[:, t * P:t * P + P], att[:, t, :], ident[:, :])
                    last.then_inc(misc_filled, 1)
                elif kind == "proj":
                    for t in range(QT):
                        last = pe.matmul(misc[:, t * D:t * D + D], aT[:, t * P:t * P + P],
                                         wts[:, WI[a.name + "_o"], :], start=True, stop=True)
                    last.then_inc(misc_filled, 1)
                elif kind == "nT":
                    pe.wait_ge(norm_ready, (n + 1).on(j))
                    for t in range(QT):
                        last = pe.transpose(misc[:, t * P:t * P + P], normed[:, par, t, :], ident[:, :])
                    last.then_inc(misc_filled, 1)

            def ff_block(ph):
                name, f = ph["name"], FF[ph["name"]]
                ybase = {"moe0": 0, "ffn": 1, "moe1": 2}.get(name, 0)
                for kind, i in FF_STEPS[name]:
                    if kind[0] == "post":
                        post_step(att_step, ph, kind[1])
                        continue
                    par = i % 2
                    if (kind, i) in FF_ORDER[name]:
                        take_misc(Lin(ph["misc"] + FF_ORDER[name].index((kind, i))), None)
                    x = fin[:, par, :]
                    if kind == "nT":
                        src = {"norm0": ft3, "moe0": ft2, "ffn": ft1}[name]
                        pe.wait_ge(f_norm, ph["fnorm"] + i + 1)
                        for t in range(BT):
                            last = pe.transpose(misc[:, t * P:t * P + P], src[:, t, :], ident[:, :])
                        last.then_inc(misc_filled, 1)
                    elif kind == "gate":
                        pe.wait_ge(fin_loaded[par], ph["fin"] + 16 * (i // 2 + 1))
                        e = f["experts"]
                        gw = gw0 if name == "moe0" else gw1
                        for t in range(BT):
                            last = pe.matmul(misc[:, t * e:t * e + e], x[:, t * P:t * P + P], gw[:, :], start=True,
                                             stop=True)
                        last.then_inc(misc_filled, 1)
                    elif kind == "spread":
                        pe.wait_ge(gate_ready, ph["gate"] + i + 1)
                        for t in range(BT):
                            if name == "moe0":
                                last = pe.transpose(misc[0:E0, :].bitcast(BF16)[:, t * P:t * P + P], ohb[:, t, :],
                                                    identb[:, :])
                            else:
                                last = pe.transpose(misc[0:E1, t * P:t * P + P], oh1[:, t, 0:E1], ident[:, :])
                        last.then_inc(misc_filled, 1)
                    elif kind == "mask0":
                        pe.wait_ge(misc_drained, ph["misc"] + FF_ORDER[name].index(("spread", i)) + 1)
                        if ph["y"] + i:
                            pe.wait_ge(y_ready, ph["y"] + i)
                        if name == "moe0":
                            pe.matmul(av_ps[:, :], b2_0[:, :], ohTf[:, :], start=True, stop=False)
                    elif isinstance(kind, tuple) and kind[0] == "mask":
                        e = kind[1]
                        mk = i * f["experts"] + e
                        if mk >= 2:
                            pe.wait_ge(gated_ready, ph["ga"] + (mk - 1) * f["tiles"])
                        if name == "moe0":
                            pe.matmul(s_ps[:, mk % 2, :], sel_b[:, e, :], ohT[:, :], start=True, stop=True) \
                                .then_inc(mask_filled, 1)
                        else:
                            pe.matmul(s_ps[:, mk % 2, :], sel_f[0:E1, e, :], ohTf[0:E1, :], start=True, stop=True) \
                                .then_inc(mask_filled, 1)
                    elif isinstance(kind, tuple) and kind[0] == "h":
                        e, t = kind[1:]
                        c = i * f["hid"] + e * f["tiles"] + t
                        if name == "moe1":
                            if c >= 2:
                                pe.wait_ge(gated_ready, ph["ga"] + c - 1)
                            pe.matmul(hid_ps[:, 2 * (c % 2), :], w1_1[:, e, t * P:t * P + P], x, start=True, stop=True)
                            pe.matmul(hid_ps[:, 2 * (c % 2) + 1, :], w3_1[:, e, t * P:t * P + P], x, start=True,
                                      stop=True).then_inc(hid_filled, 1)
                        else:
                            if name == "ffn" and t == 0:
                                pe.wait_ge(fin_loaded[par], ph["fin"] + 16 * (i // 2 + 1))
                                if ph["y"] + i:
                                    pe.wait_ge(y_ready, ph["y"] + i)
                            if c >= 4:
                                pe.wait_ge(hid_ready, ph["hid"] + c - 3)
                            w = fc1[:, t * P:t * P + P] if name == "ffn" else w1_0[:, e, t * P:t * P + P]
                            pe.matmul(hid_ps[:, c % 4, :], w, x, start=True, stop=True).then_inc(hid_filled, 1)
                    elif isinstance(kind, tuple) and kind[0] == "down":
                        e, t = kind[1:]
                        c = i * f["hid"] + e * f["tiles"] + t
                        if name == "ffn":
                            pe.wait_ge(hid_ready, ph["hid"] + c + 1)
                            w, src = fc2[:, t, :], hid[:, c % 8, :]
                        else:
                            pe.wait_ge(gated_ready, ph["ga"] + c + 1)
                            w = w2_0[:, e, t, :] if name == "moe0" else w2_1[:, e, t, :]
                            src = gated[:, c % 8, :]
                        first = e == 0 and t == 0 and name != "moe0"
                        end = e == f["experts"] - 1 and t == f["tiles"] - 1
                        mm = pe.matmul(av_ps[:, :], w, src, start=first, stop=end)
                        mm.then_inc(gated_used, 1)
                        if end:
                            pe.wait_ge(gated_used, ph["hid"] + c + 1)
                            pe.sem_inc(y_filled, 1)
                    elif kind == "back":
                        pe.wait_ge(y_ready, ph["y"] + i + 1)
                        for t in range(BT):
                            last = pe.transpose(misc[:, t * P:t * P + P], ysb[:, t * P:t * P + P], ident[:, :])
                        last.then_inc(misc_filled, 1)

            for n, ph in enumerate(plan):
                if n == 1:
                    pe.wait_ge(weights_loaded, WEIGHTS)
                if ph["name"] == "moe0":
                    pe.wait_ge(weights_loaded, WEIGHTS0)
                if ph["name"] == "ffn":
                    pe.wait_ge(weights_loaded, WEIGHTS2)
                if "att" in ph:
                    run_att(pe, ph, att_step)
                else:
                    ff_block(ph)


def ff_steps(name, experts, tiles, lag):
    out = []
    if name == "norm0":
        for i in range(NBLK):
            out += [("norm", i), ("nT", i)]
        return out

    def tail(i):
        if name == "moe1":
            return [("back", i)]
        if name == "moe0":
            return [("back", i), ("tail2", i), ("nT", i)]
        return [("back", i), ("tail2", i), ("tail3", i), ("tail4", i), ("nT", i)]

    def gate(i):
        return [("gate", i), ("choose", i), ("spread", i)] if name != "ffn" else []

    post = [(("post", k), 0) for k in range(5 if name == "ffn" else 6)]
    g0 = gate(0)
    out += g0[:1] + post[:2] + g0[1:2] + post[2:-2] + g0[2:]
    for i in range(NBLK):
        if name != "ffn":
            out.append(("mask0", i))
        work = [(e, t) for e in range(experts) for t in range(tiles)]
        extra = {} if i else {POST_AT[name][0]: post[-2:-1], POST_AT[name][1]: post[-1:]}
        if i and name != "ffn":
            t0 = tail(i - 1)
            pos = {"moe0": [3, 12, 16], "moe1": [3]}[name]
            for p, s in zip(pos, t0):
                extra.setdefault(p, []).append(s)
        if i + 1 < NBLK and name != "ffn":
            pos = {"moe0": [19, 20, 30], "moe1": [5, 6, 10]}[name]
            for p, s in zip(pos, gate(i + 1)):
                extra.setdefault(p, []).append(s)
        for n in range(len(work) + lag):
            if n < len(work):
                e, t = work[n]
                if t == 0 and name != "ffn":
                    out.append((("mask", e), i))
                out.append((("h", e, t), i))
            if n >= lag:
                out.append((("down", *work[n - lag]), i))
            out += extra.get(n, [])
        out.append(("y", i))
        if name == "ffn":
            out += [("nT", i - 1)] * (i > 0) + tail(i)[:-1]
    out += tail(NBLK - 1)[-1:] if name == "ffn" else tail(NBLK - 1)
    return out


POST_AT = {"moe0": (2, 5), "ffn": (4, 6), "moe1": (2, 5)}
FF_STEPS = {"norm0": ff_steps("norm0", 0, 0, 0), "moe0": ff_steps("moe0", E0, 4, 4), "ffn": ff_steps("ffn", 1, 4, 4),
            "moe1": ff_steps("moe1", E1, 3, 3)}
POST_USES = {"moe0": (0, 1, 2, 3, 5), "ffn": (0, 1, 4), "moe1": (0, 1, 2, 3, 5)}
FF_ORDER = {n: [s for s in st if s[0] in ("nT", "gate", "spread", "back")
                or (s[0][0] == "post" and s[0][1] in POST_USES[n])] for n, st in FF_STEPS.items()}


def kernel(**inputs):
    import concourse.bacc as bacc
    from concourse.bass_utils import run_bass_kernel_spmd

    a = {k: np.asarray(v) for k, v in inputs.items()}
    f32 = np.float32
    c = np.ascontiguousarray
    perm = np.array([h * HD + d for d in range(HD) for h in range(HEADS)])
    kv_of = np.array([(h // 4) * HD + d for d in range(HD) for h in range(HEADS)])
    swap = np.array([h * HD + (d + HD // 2) % HD for d in range(HD) for h in range(HEADS)])
    kv_swap = np.array([(h // 4) * HD + (d + HD // 2) % HD for d in range(HD) for h in range(HEADS)])
    v_of = np.array([(h // 4) * HD + d for h in range(HEADS) for d in range(HD)])
    wts = np.stack([
        a["L0_xattn_Wq"].T[:, perm], a["L0_xattn_Wk"].T[:, perm], a["L0_xattn_Wv"].T, a["L0_xattn_Wo"].T,
        a["L1_xattn_sa_wq"][:, perm], a["L1_xattn_sa_wk"][:, perm], a["L1_xattn_sa_wv"],
        a["L1_xattn_ca_wq"][:, perm], a["L1_xattn_ca_wk"][:, perm], a["L1_xattn_ca_wv"],
        a["L1_ffn_wq"][:, perm], a["L1_ffn_wq"][:, swap], a["L1_ffn_wk"][:, kv_of], a["L1_ffn_wk"][:, kv_swap],
        a["L1_ffn_wv"][:, v_of], a["L1_ffn_wo"]])
    vecs = np.stack([a["L0_xattn_bo"], a["L0_xattn_bv"], a["L1_xattn_sa_bv"], a["L1_xattn_ca_bv"],
                     a["L1_xattn_ln1_g"], a["L1_xattn_ln1_b"], a["L1_xattn_ln2_g"], a["L1_xattn_ln2_b"],
                     a["L1_xattn_ln3_g"], a["L1_xattn_ln3_b"], a["L1_ffn_g1"], a["L1_ffn_g2"]])
    cols = np.stack([a["L0_xattn_bq"][perm], a["L0_xattn_bk"][perm], a["L1_xattn_sa_bq"][perm],
                     a["L1_xattn_sa_bk"][perm], a["L1_xattn_ca_bq"][perm], a["L1_xattn_ca_bk"][perm],
                     a["L1_xattn_fc2_b"], a["L1_xattn_fc2_b"]], axis=1)
    inv = (1.0 / f32(10000.0) ** (np.arange(0, HD, 2, dtype=f32) / f32(HD))).astype(f32)
    ang = (np.arange(SQ, dtype=f32)[:, None] * inv[None, :]).astype(f32)
    ang = np.concatenate([ang, ang], axis=1)
    cos, sin = np.cos(ang).astype(f32).T, np.sin(ang).astype(f32).T
    sin = sin * np.where(np.arange(HD) < HD // 2, -1.0, 1.0).astype(f32)[:, None]
    cos, sin = np.repeat(cos, HEADS, axis=0), np.repeat(sin, HEADS, axis=0)
    ropes = np.stack([cos * f32(SCALE), sin * f32(SCALE), cos, sin], axis=1)
    i, k = np.arange(P)[:, None], np.arange(P)[None, :]
    masks = np.stack([np.where(k > i, BIG, 0.0), np.where(i > k, BIG, 0.0), np.full((P, P), BIG)], axis=1)
    sel = np.zeros((E0, E0, P), f32)
    for e in range(E0):
        sel[e, e, :] = 1.0
    host = {
        "x": c(a["x"].reshape(B * SQ, D)),
        "ctxT": c(a["ctx_1024"].transpose(0, 2, 1)),
        "g_xattn": a["g_xattn"], "g_ffn": a["g_ffn"],
        "wts": c(wts), "vecs": c(vecs), "cols": c(cols),
        "ropes": c(ropes.astype(f32)), "masks": c(masks.astype(f32)), "sel": sel,
        "ident": np.eye(P, dtype=f32), "iota": (np.arange(E0) - E0).astype(f32),
        "gw0": c(a["L0_ffn_gate_w"].T), "gb0": a["L0_ffn_gate_b"],
        "w1_0": c(a["L0_ffn_w1"].transpose(2, 0, 1)),
        "b1_0": c(a["L0_ffn_b1"].reshape(E0, H0 // P, P).transpose(2, 0, 1)),
        "w2_0": c(a["L0_ffn_w2"].transpose(2, 0, 1).reshape(H0 // P, P, E0, D).transpose(1, 2, 0, 3)),
        "b2_0": a["L0_ffn_b2"],
        "fc1": a["L1_xattn_fc1_w"], "fc1b": c(a["L1_xattn_fc1_b"].reshape(HF // P, P).T),
        "fc2": c(a["L1_xattn_fc2_w"].reshape(HF // P, P, D).transpose(1, 0, 2)),
        "w1_1": c(a["L1_ffn_w1"].transpose(1, 0, 2)), "w3_1": c(a["L1_ffn_w3"].transpose(1, 0, 2)),
        "w2_1": c(a["L1_ffn_w2"].reshape(E1, H1 // P, P, D).transpose(2, 0, 1, 3)),
        "gw1": a["L1_ffn_gate"],
    }
    nc = bacc.Bacc("TRN2", target_bir_lowering=False, num_devices=1)
    dram = {n: nc.dram_tensor(f"in_{n}", v.shape, mybir.dt.from_np(v.dtype), kind="ExternalInput").ap()
            for n, v in host.items()}
    out = nc.dram_tensor("out", (B * SQ, D), F32, kind="ExternalOutput").ap()
    program(nc, dram, [out])
    r = run_bass_kernel_spmd(nc, [{f"in_{n}": v for n, v in host.items()}], core_ids=[0])
    return r.results[0]["out"].reshape(B, SQ, D)
```
